# Optimizing a Trainium2 kernel written in Bass

```python
import numpy as np
import jax
import jax.numpy as jnp

def _softmax(x, axis=-1):
    return jax.nn.softmax(x, axis=axis)

def _gelu(x):
    return jax.nn.gelu(x, approximate=True)

def _silu(x):
    return jax.nn.silu(x)

def _sigmoid(x):
    return jax.nn.sigmoid(x)

def _layernorm(x, axis=-1, eps=1e-05):
    m = jnp.mean(x, axis=axis, keepdims=True)
    v = jnp.var(x, axis=axis, keepdims=True)
    return (x - m) / jnp.sqrt(v + eps)

def _scatter_add(tgt, idx, src, axis=0):
    return tgt.at[idx].add(src)

def _segment_sum(src, seg, n):
    return jax.ops.segment_sum(src, seg, n)
kernel_name = 'mk_macaron_d1_jaxref_r8_b13800'

def setup_inputs(seed: int=0):
    np.random.seed(seed)
    _w = jnp.asarray

    def _L0_attn_setup():
        import math
        import jax, jax.numpy as jnp
        import numpy as np
        HEADS = 16
        key = jax.random.key(seed)
        k1, k2, k3, k4, k5 = jax.random.split(key, 5)
        B, S, D = (2, 256, 128)
        return {'x': jax.random.normal(k1, (B, S, D), dtype=jnp.float32), 'Wqkv': jax.random.normal(k2, (3 * D, D), dtype=jnp.float32) * (1.0 / math.sqrt(D)), 'bqkv': jax.random.normal(k3, (3 * D,), dtype=jnp.float32) * 0.02, 'Wo': jax.random.normal(k4, (D, D), dtype=jnp.float32) * (1.0 / math.sqrt(D)), 'bo': jax.random.normal(k5, (D,), dtype=jnp.float32) * 0.02}
    _L0_attn_in = _L0_attn_setup()

    def _L0_ffn_setup():
        import jax, jax.numpy as jnp
        import numpy as np
        D_MODEL = 128
        D_MLP = 512
        N_EXPERTS = 8
        TOP_K = 2
        BATCH = 1
        POS = 256
        key = jax.random.key(seed)
        k0, k1, k2, k3, k4 = jax.random.split(key, 5)
        s = 0.02
        x = jax.random.normal(k0, (BATCH, POS, D_MODEL), jnp.float32)
        W_gate = jax.random.normal(k1, (D_MODEL, N_EXPERTS), jnp.float32) * s
        We_gate = jax.random.normal(k2, (N_EXPERTS, D_MODEL, D_MLP), jnp.float32) * s
        We_in = jax.random.normal(k3, (N_EXPERTS, D_MODEL, D_MLP), jnp.float32) * s
        We_out = jax.random.normal(k4, (N_EXPERTS, D_MLP, D_MODEL), jnp.float32) * s
        return {'x': x, 'W_gate': W_gate, 'We_gate': We_gate, 'We_in': We_in, 'We_out': We_out}
    _L0_ffn_in = _L0_ffn_setup()
    _d = {'L0_attn_x': _L0_attn_in['x'], 'L0_attn_Wqkv': _L0_attn_in['Wqkv'], 'L0_attn_bqkv': _L0_attn_in['bqkv'], 'L0_attn_Wo': _L0_attn_in['Wo'], 'L0_attn_bo': _L0_attn_in['bo'], 'L0_ffn_W_gate': _L0_ffn_in['W_gate'], 'L0_ffn_We_gate': _L0_ffn_in['We_gate'], 'L0_ffn_We_in': _L0_ffn_in['We_in'], 'L0_ffn_We_out': _L0_ffn_in['We_out']}
    _x0 = _d['L0_attn_x']
    _d['L0_attn_x'] = jax.random.normal(jax.random.fold_in(jax.random.key(seed), 1), (4, 512, 128), dtype=_x0.dtype)
    del _x0
    return _d

def reference(L0_attn_x, L0_attn_Wqkv, L0_attn_bqkv, L0_attn_Wo, L0_attn_bo, L0_ffn_W_gate, L0_ffn_We_gate, L0_ffn_We_in, L0_ffn_We_out):

    def _L0_attn_ref(x, Wqkv, bqkv, Wo, bo):
        import math
        import jax, jax.numpy as jnp
        import numpy as np
        HEADS = 16
        B, S, D = x.shape
        H = HEADS
        hd = D // H
        qkv = x @ Wqkv.T + bqkv
        qkv = qkv.reshape(B, H, S, 3 * hd)
        q, k, v = jnp.split(qkv, 3, axis=-1)
        scores = jnp.einsum('bhsd,bhtd->bhst', q, k) * (1.0 / math.sqrt(hd))
        attn = jax.nn.softmax(scores, axis=-1)
        vals = jnp.einsum('bhst,bhtd->bhsd', attn, v)
        vals = vals.reshape(B, S, D)
        return vals @ Wo.T + bo

    def _L0_ffn_ref(x, W_gate, We_gate, We_in, We_out):
        import jax, jax.numpy as jnp
        import numpy as np
        D_MODEL = 128
        D_MLP = 512
        N_EXPERTS = 8
        TOP_K = 2
        BATCH = 1
        POS = 256
        B, P, D = x.shape
        T = B * P
        E = W_gate.shape[1]
        h = x.reshape(T, D)
        logits = h @ W_gate
        probs = jax.nn.softmax(logits.astype(jnp.float32), axis=-1)
        topw, topi = jax.lax.top_k(probs, TOP_K)
        topw = topw / jnp.sum(topw, axis=-1, keepdims=True)
        topw = topw.astype(x.dtype)
        w_full = jnp.zeros((T, E), x.dtype).at[jnp.arange(T)[:, None], topi].add(topw)

        def per_expert(acc, params):
            Wg, Wi, Wo, we = params
            hid = jax.nn.silu(h @ Wg) * (h @ Wi)
            return (acc + hid @ Wo * we[:, None], None)
        res, _ = jax.lax.scan(per_expert, jnp.zeros((T, D), x.dtype), (We_gate, We_in, We_out, w_full.T))
        return res.reshape(B, P, D)
    x = L0_attn_x
    x = x + 0.5 * _L0_ffn_ref(_layernorm(x, axis=-1), L0_ffn_W_gate, L0_ffn_We_gate, L0_ffn_We_in, L0_ffn_We_out)
    x = x + _L0_attn_ref(_layernorm(x, axis=-1), L0_attn_Wqkv, L0_attn_bqkv, L0_attn_Wo, L0_attn_bo)
    x = x + 0.5 * _L0_ffn_ref(_layernorm(x, axis=-1), L0_ffn_W_gate, L0_ffn_We_gate, L0_ffn_We_in, L0_ffn_We_out)
    return x

_drawn_inputs = setup_inputs


def setup_inputs(seed=0):
    import zlib

    import numpy as np

    out = dict(_drawn_inputs(seed))
    spreads = {}
    factors = {'L0_attn_bqkv': 5.671,
     'L0_attn_bo': 2.837,
     'L0_ffn_W_gate': 8.0,
     'L0_ffn_We_gate': 7.041,
     'L0_ffn_We_in': 7.02,
     'L0_ffn_We_out': 7.017}
    for name, (base, spread) in spreads.items():
        noise = np.random.default_rng([zlib.crc32(name.encode()), seed]).standard_normal(out[name].shape)
        drawn = base * np.exp(spread * noise) if base else spread * noise
        out[name] = jnp.asarray(drawn.astype(out[name].dtype))
    for name, factor in factors.items():
        out[name] = (out[name] * factor).astype(out[name].dtype)
    return out
```

```python
import concourse.bass as bass
from concourse import mybir
from contextlib import ExitStack

B, S, D = 4, 512, 128
HEADS, HD = 16, 8
F, E = 512, 8
P = 128
TILES = B * S // P
SLOTS = -(-(2 * TILES + E - 1) // 4) * 4
BLK = S // HEADS
NB = P // BLK
G = D // HD
GC = P // BLK
NC = G // GC
KROWS = 3 * HD
WE = 3072
EPS = 1e-5


def tile_no(it, c):
    return c if it is None else it * 4 + c


def half_no(it, c):
    return c // 2 if it is None else it * 2 + c // 2


def quarter_no(it, c):
    return c // 4 if it is None else it + c // 4


def wait(eng, sem, value):
    if isinstance(value, int) and value <= 0:
        return
    eng.wait_ge(sem, value)


def wait_apart(eng, sem, value, ready):
    value = value if isinstance(value, int) else eng.snap(value)
    eng.wait_ge(ready, 1)
    eng.wait_ge(sem, value)


def macaron_kernel(nc, x_in, w_gate_up, w_down, w_att, w_router, b_qk, b_v, b_o, out,
                   slot_x, slot_y, qk_hop, max_hop, att_hop):
    f32, f32r, bf16 = mybir.dt.float32, mybir.dt.float32r, mybir.dt.bfloat16
    i32, u32 = mybir.dt.int32, mybir.dt.uint32
    ALU = mybir.AluOpType
    ACT = mybir.ActivationFunctionType
    X = mybir.AxisListType.X
    ds = bass.ds

    ctx = ExitStack()
    with ctx:
        def sb(name, shape, dt=f32):
            return ctx.enter_context(nc.sbuf_tensor(name, shape, dt))

        def ps(name, shape):
            return ctx.enter_context(nc.psum_tensor(name, shape, f32))

        def sem(name):
            return ctx.enter_context(nc.semaphore(name))

        x_sb = sb("x_sb", [P, TILES, D])
        xn_all = sb("xn_all", [P, TILES, D])
        w_exp = sb("w_exp", [P, E, WE], f32r)
        big = sb("big", [P, 8192])
        stack = sb("stack", [P, 4096], f32r)
        xT_split = sb("xT_split", [P, 1536], f32r)
        w_small = sb("w_small", [P, 4 * D + E])
        w_qk = sb("w_qk", [P, 2, 2, D], f32r)
        w_o = sb("w_o", [P, 2 * D], f32r)
        w_r = sb("w_r", [P, 2 * E], f32r)
        bqk_sb = sb("bqk_sb", [P, 2])
        bv_sb = sb("bv_sb", [P, NC * HD])
        bo_sb = sb("bo_sb", [P, D])
        ident = sb("ident", [P, P])
        upper = sb("upper", [P, P], bf16)
        ones_b = sb("ones_b", [P, P], bf16)
        rev = sb("rev", [P, E])
        thr = sb("thr", [P, TILES])
        slot_j = sb("slot_j", [1, SLOTS])
        before = sb("before", [P, E, E])
        halves = sb("halves", [P, 12])
        carrier = sb("carrier", [P, 1])
        st6 = sb("st6", [P, TILES, 6])
        mv = sb("mv", [P, TILES, 2])
        rs = sb("rs", [P, TILES, 4])
        lgB = sb("lgB", [P, 4, E])
        lg = sb("lg", [P, TILES, E])
        r1 = sb("r1", [P, TILES, E])
        r2 = sb("r2", [P, TILES, E])
        one1 = sb("one1", [P, TILES, E])
        one2 = sb("one2", [P, TILES, E])
        sel = sb("sel", [P, TILES, E], bf16)
        m1 = sb("m1", [P, TILES])
        m2 = sb("m2", [P, TILES])
        kk = sb("kk", [P, TILES])
        e2 = sb("e2", [P, TILES])
        n_e = sb("n_e", [P, E])
        cmp = sb("cmp", [P, E, TILES])
        sl_e = sb("sl_e", [P, E])
        off = sb("off", [P, E])
        offs = sb("offs", [P, E])
        incl = sb("incl", [P, E])
        mm = sb("mm", [P, E, E])
        se = sb("se", [1, SLOTS, E])
        sef = sb("sef", [1, SLOTS])
        slot_w = sb("slot_w", [1, SLOTS], i32)
        posf = sb("posf", [P, TILES, 2])
        pos = sb("pos", [P, TILES, 2], u32)
        wts = sb("wts", [P, TILES, 2])
        pos_now = sb("pos_now", [P, 2, 2], u32)
        yg = sb("yg", [P, 2, 2, D])
        xn_t = sb("xn_t", [P, 2, D])
        xa_f = sb("xa_f", [P, P])
        xa = sb("xa", [P, 2, P], f32r)
        qk_hl = sb("qk_hl", [P, 2, 2, P], f32r)
        v_st = sb("v_st", [P, 4, NB, NC, 32])
        mx = sb("mx", [P, 2, NB * NC])
        neg_m = sb("neg_m", [NB * NC, P], f32r)
        o_sb = sb("o_sb", [P, S])
        nd = sb("nd", [P, 2, P])
        vals = sb("vals", [P, P])
        vh = sb("vh", [P, 2, P], f32r)
        oB = sb("oB", [P, P])
        oA = sb("oA", [P, P])
        yB = sb("yB", [P, D])

        stage = big[:, 0:4 * 1536].rearrange("p (r c) -> p r c", r=4)
        zeros = big[:, 6144:8192]
        xg = big[:, 0:512].rearrange("p (r c) -> p r c", r=4)
        s_act = big[:, 512:1536].rearrange("p (r c) -> p r c", r=2)
        h_act = big[:, 1536:2560].rearrange("p (r c) -> p r c", r=2)
        y_out = big[:, 2560:2816].rearrange("p (r c) -> p r c", r=2)
        prob = big[:, :].rearrange("p (a b c s) -> p a b c s", a=2, b=NB, c=2)
        hT_h = stack[:, 0:1024].rearrange("p (r c) -> p r c", r=2)
        hT_l = stack[:, 1024:2048].rearrange("p (r c) -> p r c", r=2)
        xg_h = xT_split[:, 0:256].rearrange("p (r c) -> p r c", r=2)
        xg_l = xT_split[:, 256:512].rearrange("p (r c) -> p r c", r=2)
        xr_h = xT_split[:, 512:1024]
        xr_l = xT_split[:, 1024:1536]
        def q_st(r, rows=KROWS + 1):
            return stack[32 * r:32 * r + rows, 0:2048].rearrange("p (b s) -> p b s", b=NB)

        def k_st(r, rows=KROWS + 1):
            return stack[32 * r:32 * r + rows, 2048:4096].rearrange("p (b s) -> p b s", b=NB)

        S0 = ps("S0", [P, 512])
        S1 = ps("S1", [P, 512])
        ST0 = ps("ST0", [P, 1024])
        ST1 = ps("ST1", [P, 1024])
        PVB = ps("PVB", [P, 512])
        MISC = ps("MISC", [P, 512])
        SB = [S0, S1]
        ST = [ST0, ST1]
        gate_p = [S0[:, :], S1[:, :]]
        up_p = [ST0[:, 0:512], ST0[:, 512:1024]]
        hT_p = [ST1[:, 0:512], ST1[:, 512:1024]]
        xg_p = PVB[:, 0:P]
        y_p = MISC[:, 0:2 * D]

        x_loaded, small_loaded, w_raw = sem("x_loaded"), sem("small_loaded"), [sem(f"w_raw{i}") for i in range(4)]
        zero_ready, zeroed = sem("zero_ready"), sem("zeroed")
        const_ready, pool_step = sem("const_ready"), sem("pool_step")
        w_hi_done, w_lo_done = sem("w_hi_done"), sem("w_lo_done")
        small_hi, small_done = sem("small_hi"), sem("small_done")
        dve_step = sem("dve_step")

        class Phase:
            def __init__(self, f):
                self.stats, self.rstd, self.xn, self.xT = (
                    sem(f"stats_{f}"), sem(f"rstd_{f}"), sem(f"xn_{f}"), sem(f"xT_{f}"))
                self.xhi, self.xlo, self.logit, self.lgB = (
                    sem(f"xhi_{f}"), sem(f"xlo_{f}"), sem(f"logit_{f}"), sem(f"lgB_{f}"))
                self.lg, self.gap, self.exp2, self.sel = (
                    sem(f"lg_{f}"), sem(f"gap_{f}"), sem(f"exp2_{f}"), sem(f"sel_{f}"))
                self.rank, self.pos, self.slotw, self.sent = (
                    sem(f"rank_{f}"), sem(f"pos_{f}"), sem(f"slotw_{f}"), sem(f"sent_{f}"))
                self.xgT, self.xgh, self.xgl, self.gate = (
                    sem(f"xgT_{f}"), sem(f"xgh_{f}"), sem(f"xgl_{f}"), sem(f"gate_{f}"))
                self.up, self.silu, self.h, self.hT = (
                    sem(f"up_{f}"), sem(f"silu_{f}"), sem(f"h_{f}"), sem(f"hT_{f}"))
                self.hTh, self.hTl, self.outp, self.yB = (
                    sem(f"hTh_{f}"), sem(f"hTl_{f}"), sem(f"outp_{f}"), sem(f"yB_{f}"))
                self.y, self.half, self.combined, self.pos_now = (
                    sem(f"y_{f}"), sem(f"half_{f}"), sem(f"combined_{f}"), sem(f"pos_now_{f}"))
                self.xg = [sem(f"xg{r}_{f}") for r in range(4)]
                self.stored = [sem(f"stored{r}_{f}") for r in range(2)]
                self.gathered = [sem(f"gathered{r}_{f}") for r in range(2)]

        ffn = [Phase(0), Phase(1)]
        a_stats, a_rstd, a_xn, a_xT, a_xah, a_xaf, a_xal = map(sem, (
            "a_stats", "a_rstd", "a_xn", "a_xT", "a_xah", "a_xaf", "a_xal"))
        a_qkv, a_qkh, a_qkl, a_v = map(sem, ("a_qkv", "a_qkh", "a_qkl", "a_v"))
        a_hop = sem("a_hop")
        a_stacked = [sem(f"a_stacked{r}") for r in range(4)]
        a_s, a_max = sem("a_s"), sem("a_max")
        a_mT, a_negm, a_mhop = sem("a_mT"), sem("a_negm"), sem("a_mhop")
        a_mrow = [sem(f"a_mrow{r}") for r in range(4)]
        a_st, a_exp, a_pv, a_o = sem("a_st"), sem("a_exp"), sem("a_pv"), sem("a_o")
        a_ohop, a_nd = sem("a_ohop"), sem("a_nd")
        a_vals, a_vh, a_vl, a_op, a_oB, a_oA, a_x = map(sem, (
            "a_vals", "a_vh", "a_vl", "a_op", "a_oB", "a_oA", "a_x"))
        stored_out = sem("stored_out")
        a_pool_step, a_ob, a_bn, a_rec = map(sem, ("a_pool_step", "a_ob", "a_bn", "a_rec"))

        class Steps:
            def __init__(self, eng, s):
                self.eng, self.s, self.n = eng, s, 0

            def link(self, ins):
                self.n += 1
                ins.then_inc(self.s, 1)
                self.eng.wait_ge(self.s, self.n)

        def sync_program(sp):
            sp.dma_start(x_sb[:, :, :], x_in.rearrange("(n p) d -> p n d", p=P)).then_inc(x_loaded, 16)
            sp.dma_start(w_small[:, :], w_att).then_inc(small_loaded, 16)
            sp.dma_start(bqk_sb[:, :], b_qk).then_inc(small_loaded, 16)
            sp.dma_start(bv_sb[:, :], b_v).then_inc(small_loaded, 16)
            sp.dma_start(bo_sb[:, :], b_o).then_inc(small_loaded, 16)
            for e in range(E):
                r = e % 4
                wait(sp, w_lo_done, e - 3)
                sp.dma_start(stage[:, r, 0:1024].rearrange("p (k f) -> p k f", k=2),
                             w_gate_up[e:e + 1].rearrange("e k p f -> p (e k) f")).then_inc(w_raw[r], 16)
                sp.dma_start(stage[:, r, 1024:1536].rearrange("p (c d) -> p c d", c=4),
                             w_down[e:e + 1].rearrange("e (c p) d -> p (e c) d", p=P)).then_inc(w_raw[r], 16)

            sp.wait_ge(zero_ready, 1)
            for a in range(0, SLOTS, 8):
                sp.dma_start(slot_x[a * P:(a + 8) * P, :].rearrange("(n p) d -> p n d", p=P),
                             zeros[:, 0:1024].rearrange("p (n d) -> p n d", d=D)).then_inc(zeroed, 16)
            slots_sp(sp, 0)
            attention_sp(sp)
            slots_sp(sp, 1)
            q = ffn[1]
            with sp.Fori(0, TILES // 4) as it:
                sp.wait_ge(q.combined, it * 4 + 4)
                sp.dma_start(out.rearrange("(n p) d -> p n d", p=P)[:, ds(it * 4, 4), :],
                             x_sb[:, ds(it * 4, 4), :]).then_inc(stored_out, 16)
            sp.wait_ge(stored_out, 16 * (TILES // 4))

        def slots_sp(sp, f):
            q = ffn[f]

            def load(it, c):
                j, r = tile_no(it, c), c % 4
                wait(sp, q.xgT, j - 3 if not isinstance(j, int) or j >= 4 else 0)
                sp.dma_start(xg[:, r, :], slot_x[ds(j * P, P), :]).then_inc(q.xg[r], 16)

            def store(it, c):
                j, r = tile_no(it, c), c % 2
                sp.wait_ge(q.y, j + 1)
                sp.dma_start(slot_y[ds(j * P, P), :], y_out[:, r, :]).then_inc(q.stored[r], 16)

            sp.wait_ge(q.sent, 16 * 2 * TILES)
            if f == 0:
                sp.wait_ge(w_lo_done, E)
            else:
                sp.wait_ge(a_pv, 2 * TILES)
            for c in range(4):
                load(None, c)
            with sp.Fori(0, SLOTS // 4 - 1) as it:
                for c in range(4):
                    load(it, c + 4)
                    store(it, c)
            for c in range(4):
                store(None, SLOTS - 4 + c)
            if f == 0:
                pass

        def attention_sp(sp):
            def stack_in(it, c):
                n, r = tile_no(it, c), c % 4
                sp.wait_ge(a_qkl, n + 1)
                sp.dma_start(qk_hop.rearrange("a p t -> p a t"),
                             qk_hl[:, :, :, :].rearrange("p h k (b t) -> p (h k b) t", t=BLK).bitcast(f32))\
                    .then_inc(a_hop, 16)
                sp.wait_ge(a_hop, n * 16 + 16)
                wait(sp, a_st, n * 8 - 24 if not isinstance(n, int) or n >= 4 else 0)
                src = qk_hop.rearrange("(h k b) (d g) t -> h k d b (g t)", h=2, k=2, d=HD)
                for part, (qs, ks) in enumerate(((0, 0), (1, 0), (0, 1))):
                    for dst, k, s in ((q_st, 0, qs), (k_st, 1, ks)):
                        sp.dma_start(stack_rows(dst, r, part).bitcast(f32), src[s, k]).then_inc(a_stacked[r], 16)

            def stack_rows(which, r, part):
                base = 0 if which is q_st else 2048
                return stack[32 * r + part * HD:32 * r + (part + 1) * HD, base:base + 2048].rearrange(
                    "p (b s) -> p b s", b=NB)

            def max_in(it, c):
                n, r = tile_no(it, c), c % 4
                sp.wait_ge(a_negm, n + 1)
                sp.dma_start(max_hop, neg_m[:, :].bitcast(f32)).then_inc(a_mhop, 16)
                sp.wait_ge(a_mhop, n * 16 + 16)
                row = stack[32 * r + KROWS:32 * r + KROWS + 1, 0:2048]
                sp.dma_start(row.bitcast(f32), max_hop.rearrange("(o a) s -> o (a s)", o=1)).then_inc(a_mrow[r], 16)

            def out_hop(it, c):
                n = tile_no(it, c)
                sp.wait_ge(a_o, n + 1)
                sp.dma_start(att_hop, o_sb[:, :]).then_inc(a_ohop, 16)
                sp.wait_ge(a_ohop, n * 16 + 16)
                wait(sp, a_vals, n)
                src = att_hop.rearrange("(b k d) (g t) -> k (d g) b t", b=NB, k=4, g=G)
                for k in range(2):
                    sp.dma_start(nd[:, k, :].rearrange("p (b t) -> p b t", b=NB), src[k]).then_inc(a_nd, 16)

            def turn(it, c, i=None):
                i = c if it is None else None
                ok = lambda n: it is not None or 0 <= n < TILES
                if ok(c - 1):
                    out_hop(it, c - 1)
                if ok(c + 1):
                    max_in(it, c + 1)
                if ok(c + 3):
                    stack_in(it, c + 3)

            for_turns(sp, turn)

        def for_turns(eng, turn):
            for c in range(-3, 1):
                turn(None, c)
            with eng.Fori(0, 3) as it:
                for c in range(1, 5):
                    turn(it, c)
            for c in range(13, 17):
                turn(None, c)

        def gpsimd_program(pool):
            st = Steps(pool, pool_step)
            pool.memset(zeros, 0.0).then_inc(zero_ready, 1)
            st.link(pool.memset(ident[:, :], 0.0))
            pool.memset(ones_b[:, :], 1.0)
            st.link(pool.memset(before[:, :, :], 1.0))
            for k, value in enumerate((-0.5, 1.5, EPS)):
                pool.memset(halves[:, 4 * k:4 * k + 4], value)
            pool.memset(v_st[:, :, :, :, :], 1.0)
            st.link(pool.memset(stack[:, 2048:4096].bitcast(f32), 1.0))
            pool.affine_select(out=ident[:, :], in_=ident[:, :], compare_op=ALU.not_equal, fill=1.0,
                               base=0, pattern=[[-1, P]], channel_multiplier=1)
            pool.affine_select(out=upper[:, :], in_=ones_b[:, :], compare_op=ALU.is_gt, fill=0.0,
                               base=0, pattern=[[1, P]], channel_multiplier=-1)
            pool.affine_select(out=before[:, :, :], in_=before[:, :, :], compare_op=ALU.is_gt, fill=0.0,
                               base=0, pattern=[[1, E], [-1, E]], channel_multiplier=0)
            pool.iota(rev[:, :], pattern=[[-1, E]], base=E, channel_multiplier=0,
                      allow_small_or_imprecise_dtypes=True)
            pool.iota(thr[:, :], pattern=[[P, TILES]], base=0, channel_multiplier=0,
                      allow_small_or_imprecise_dtypes=True)
            pool.iota(slot_j[:, :], pattern=[[1, SLOTS]], base=0, channel_multiplier=0,
                      allow_small_or_imprecise_dtypes=True).then_inc(const_ready, 1)
            pool.wait_ge(const_ready, 1)

            for f in range(2):
                route_pool(pool, st, f)
                if f == 0:
                    pool.wait_ge(zeroed, 16 * (SLOTS // 8))
                scatter_pool(pool, f)
                if f == 0:
                    attention_pool(pool, st)
            q = ffn[1]
            for r in range(2):
                pool.wait_ge(q.stored[r], 16 * SLOTS // 2)
            for c in range(2):
                gather(pool, 1, c, 1, c)
            with pool.Fori(1, TILES // 2) as it:
                for c in range(2):
                    gather(pool, 1, it * 2 + c, it + 1, c)

        def rstd_chain(pool, link, m, r):
            c = [halves[:, k * 4:k * 4 + m.shape[1]] for k in range(3)]
            link(pool.tensor_tensor(out=r[:, :, 1], in0=m[:, :, 1], in1=c[2], op=ALU.add))
            link(pool.tensor_tensor(out=r[:, :, 0], in0=r[:, :, 1], in1=c[0], op=ALU.pow))
            link(pool.tensor_tensor(out=r[:, :, 2], in0=r[:, :, 0], in1=r[:, :, 0], op=ALU.mult))
            link(pool.tensor_tensor(out=r[:, :, 2], in0=r[:, :, 2], in1=r[:, :, 1], op=ALU.mult))
            link(pool.tensor_tensor(out=r[:, :, 2], in0=r[:, :, 2], in1=c[0], op=ALU.mult))
            link(pool.tensor_tensor(out=r[:, :, 2], in0=r[:, :, 2], in1=c[1], op=ALU.add))
            return pool.tensor_tensor(out=r[:, :, 3], in0=r[:, :, 2], in1=r[:, :, 0], op=ALU.mult)

        def route_pool(pool, st, f):
            q = ffn[f]
            for i in range(TILES // 4):
                pool.wait_ge(q.stats, i + 1)
                rstd_chain(pool, st.link, mv[:, 4 * i:4 * i + 4, :], rs[:, 4 * i:4 * i + 4, :]).then_inc(q.rstd, 1)

        def scatter_pool(pool, f):
            q = ffn[f]
            pool.wait_ge(q.pos, 1)
            for n in range(TILES):
                for k in range(2):
                    pool.indirect_dma_start(slot_x, bass.IndirectOffsetOnAxis(ap=pos[:, n, k:k + 1], axis=0),
                                            xn_all[:, n, :], None).then_inc(q.sent, 16)

        def gather(pool, f, n, turn_no, r):
            q = ffn[f]
            wait(pool, q.combined, n - 1)
            pool.tensor_copy(out=pos_now[:, r, :], in_=pos[:, ds(n, 1), :].rearrange("p a k -> p (a k)"))\
                .then_inc(q.pos_now, 1)
            pool.wait_ge(q.pos_now, n + 1)
            pool.tensor_tensor(out=carrier[:, :], in0=halves[:, 0:1], in1=halves[:, 0:1], op=ALU.add)
            for k in range(2):
                pool.indirect_dma_start(yg[:, r, k, :], None, slot_y,
                                        bass.IndirectOffsetOnAxis(ap=pos_now[:, r, k:k + 1], axis=0))\
                    .then_inc(q.gathered[r], 16)

        def attention_pool(pool, st):
            q = ffn[0]
            for r in range(2):
                pool.wait_ge(q.stored[r], 16 * SLOTS // 2)

            def rest(it, c):
                n = tile_no(it, c)
                pool.wait_ge(a_stats, n + 1)
                steps = [0]

                def link(ins):
                    steps[0] += 1
                    ins.then_inc(a_pool_step, 1)
                    pool.wait_ge(a_pool_step, n * 6 + steps[0])
                rstd_chain(pool, link, mv[:, 0:1, :], rs[:, 0:1, :]).then_inc(a_rstd, 1)

            def residual(it, c):
                n = tile_no(it, c)
                pool.wait_ge(a_oA, n + 1)
                xt = x_sb[:, ds(n, 1), :].rearrange("p a d -> p (a d)")
                pool.tensor_tensor(out=oA[:, :], in0=oA[:, :], in1=bo_sb[:, :], op=ALU.add).then_inc(a_ob, 1)
                pool.wait_ge(a_ob, n + 1)
                pool.tensor_tensor(out=xt, in0=xt, in1=oA[:, :], op=ALU.add).then_inc(a_x, 1)

            def turn(it, c):
                ok = lambda n: it is not None or 0 <= n < TILES
                if ok(c + 3):
                    gather(pool, 0, tile_no(it, c + 3), half_no(it, c + 3) + 1, (c + 3) % 2)
                    rest(it, c + 3)
                if ok(c - 1):
                    residual(it, c - 1)
            for_turns(pool, turn)

        def scalar_program(act):
            act.wait_ge(small_loaded, 64)
            act.activation(w_qk[:, :, 0, :], w_small[:, 0:2 * D].rearrange("p (k d) -> p k d", k=2), ACT.Copy).then_inc(small_hi, 1)
            act.activation(w_o[:, 0:D], w_small[:, 2 * D:3 * D], ACT.Copy).then_inc(small_hi, 1)
            act.activation(w_r[:, 0:E], w_small[:, 4 * D:4 * D + E], ACT.Copy).then_inc(small_hi, 1)
            for f in range(2):
                route_act(act, f)
                if f == 0:
                    with act.Fori(0, E // 4) as it:
                        for r in range(4):
                            act.wait_ge(w_raw[r], it * 32 + 32)
                            we = w_exp[:, ds(it * 4 + r, 1), :].rearrange("p a c -> p (a c)")
                            act.activation(we[:, 0:2048].rearrange("p (k h f) -> p k h f", k=2, h=2)[:, :, 0, :],
                                           stage[:, r, 0:1024].rearrange("p (k f) -> p k f", k=2), ACT.Copy)
                            act.activation(we[:, 2048:3072].rearrange("p (c h d) -> p c h d", c=4, h=2)[:, :, 0, :],
                                           stage[:, r, 1024:1536].rearrange("p (c d) -> p c d", c=4), ACT.Copy).then_inc(w_hi_done, 1)
                slots_act(act, f)
                if f == 0:
                    attention_act(act)

        def route_act(act, f):
            q = ffn[f]
            for i in range(TILES // 4):
                act.wait_ge(q.xT, i + 1)
                wait(act, q.logit, i)
                act.activation(xr_h, S0[:, :], ACT.Copy).then_inc(q.xhi, 1)
                act.wait_ge(q.logit, i + 1)
                wait(act, q.lg, i)
                act.activation(lgB[:, :, :], S1[:, 0:64].rearrange("p (k h e) -> p k h e", k=4, h=2)[:, :, 1, :],
                               ACT.Copy).then_inc(q.lgB, 1)
            act.wait_ge(q.gap, 1)
            act.activation(e2[:, :], e2[:, :], ACT.Exp).then_inc(q.exp2, 1)

        def slots_act(act, f):
            q = ffn[f]

            def turn(it, c):
                ok = lambda n: it is not None or 0 <= n < SLOTS
                j = tile_no(it, c)
                if ok(c + 1):
                    act.wait_ge(q.xgT, j + 2)
                    wait(act, q.up, j)
                    act.activation(xg_h[:, (c + 1) % 2, :], xg_p, ACT.Copy).then_inc(q.xgh, 1)
                if ok(c):
                    act.wait_ge(q.gate, j + 1)
                    wait(act, q.h, j - 1)
                    act.activation(s_act[:, c % 2, :], gate_p[c % 2], ACT.Silu).then_inc(q.silu, 1)
                if ok(c - 1):
                    act.wait_ge(q.hT, j)
                    wait(act, q.outp, j - 2)
                    act.activation(hT_h[:, (c - 1) % 2, :], hT_p[(c - 1) % 2], ACT.Copy).then_inc(q.hTh, 1)
                if ok(c - 2):
                    act.wait_ge(q.outp, j - 1)
                    wait(act, q.y, j - 2)
                    act.activation(yB[:, :], y_p[:, D:2 * D], ACT.Copy).then_inc(q.yB, 1)
            slot_turns(act, turn)

        def slot_turns(eng, turn):
            for c in range(-1, 4):
                turn(None, c)
            with eng.Fori(0, SLOTS // 4 - 2) as it:
                for c in range(4, 8):
                    turn(it, c)
            for c in range(SLOTS - 4, SLOTS + 2):
                turn(None, c)

        def attention_act(act):
            def exps(it, c, k):
                n, cp, b = tile_no(it, c), k // NB, k % NB
                act.wait_ge(a_st, n * 8 + k + 1)
                wait(act, a_pv, n * 2 + cp - 1)
                act.activation(prob[:, cp, b, :, :].rearrange("p c s -> p (c s)"), ST[k % 2][:, :], ACT.Exp,
                               scale=HD ** -0.5).then_inc(a_exp, 1)

            def negm(it, c):
                n = tile_no(it, c)
                act.wait_ge(a_mT, n + 1)
                wait(act, a_mhop, n * 16)
                act.activation(neg_m[:, :], MISC[0:NB * NC, 0:P], ACT.Copy, scale=-1.0).then_inc(a_negm, 1)

            def xa_evac(it, c):
                n = tile_no(it, c)
                act.wait_ge(a_xT, n + 1)
                wait(act, a_qkv, n)
                act.activation(xa_f[:, :], MISC[:, 0:P], ACT.Copy).then_inc(a_xaf, 1)
                act.activation(xa[:, 0, :], MISC[:, 0:P], ACT.Copy).then_inc(a_xah, 1)

            def qk_evac(it, c):
                n = tile_no(it, c)
                act.wait_ge(a_qkv, n + 1)
                wait(act, a_hop, n * 16)
                for k in range(2):
                    ins = act.activation(qk_hl[:, 0, k, :], MISC[:, P * (k + 1):P * (k + 2)], ACT.Identity,
                                         bias=bqk_sb[:, k:k + 1])
                ins.then_inc(a_qkh, 1)

            def o_evac(it, c):
                n = tile_no(it, c)
                act.wait_ge(a_pv, n * 2 + 2)
                wait(act, a_ohop, n * 16)
                act.activation(o_sb[:, :], PVB[:, :], ACT.Copy).then_inc(a_o, 1)

            def vals_hi(it, c):
                n = tile_no(it, c)
                act.wait_ge(a_vals, n + 1)
                wait(act, a_op, n)
                act.activation(vh[:, 0, :], vals[:, :], ACT.Copy).then_inc(a_vh, 1)

            def op_evac(it, c):
                n = tile_no(it, c)
                act.wait_ge(a_op, n + 1)
                wait(act, a_oA, n)
                act.activation(oB[:, :], MISC[:, P:2 * P], ACT.Copy).then_inc(a_oB, 1)

            def turn(it, c):
                ok = lambda n: it is not None or 0 <= n < TILES
                for k in range(8):
                    if ok(c):
                        exps(it, c, k)
                    if k == 1 and ok(c + 1):
                        negm(it, c + 1)
                    if k == 2 and ok(c - 1):
                        o_evac(it, c - 1)
                    if k == 3 and ok(c + 3):
                        xa_evac(it, c + 3)
                    if k == 5 and ok(c + 3):
                        qk_evac(it, c + 3)
                if ok(c - 1):
                    vals_hi(it, c - 1)
                    op_evac(it, c - 1)
            for_turns(act, turn)

        def vector_program(dve):
            st = Steps(dve, dve_step)
            dve.wait_ge(const_ready, 1)
            for f in range(2):
                norm_dve(dve, st, f)
                if f == 0:
                    dve.wait_ge(small_hi, 3)
                    dve.tensor_tensor(w_qk[:, :, 1, :], w_small[:, 0:2 * D].rearrange("p (k d) -> p k d", k=2),
                                      w_qk[:, :, 0, :].bitcast(f32), ALU.subtract)
                    dve.tensor_tensor(w_o[:, D:2 * D], w_small[:, 2 * D:3 * D], w_o[:, 0:D].bitcast(f32), ALU.subtract)
                    dve.tensor_tensor(w_r[:, E:2 * E], w_small[:, 4 * D:4 * D + E], w_r[:, 0:E].bitcast(f32),
                                      ALU.subtract).then_inc(small_done, 1)
                route_dve(dve, st, f)
                if f == 0:
                    with dve.Fori(0, E // 4) as it:
                        for r in range(4):
                            dve.wait_ge(w_hi_done, it * 4 + r + 1)
                            we = w_exp[:, ds(it * 4 + r, 1), :].rearrange("p a c -> p (a c)")
                            gu = we[:, 0:2048].rearrange("p (k h f) -> p k h f", k=2, h=2)
                            dn = we[:, 2048:3072].rearrange("p (c h d) -> p c h d", c=4, h=2)
                            dve.tensor_tensor(gu[:, :, 1, :], stage[:, r, 0:1024].rearrange("p (k f) -> p k f", k=2),
                                              gu[:, :, 0, :].bitcast(f32), ALU.subtract)
                            dve.tensor_tensor(dn[:, :, 1, :], stage[:, r, 1024:1536].rearrange("p (c d) -> p c d", c=4),
                                              dn[:, :, 0, :].bitcast(f32), ALU.subtract).then_inc(w_lo_done, 1)
                slots_dve(dve, f)
                if f == 0:
                    attention_dve(dve)
            q = ffn[1]
            with dve.Fori(0, TILES // 2) as it:
                for c in range(2):
                    combine(dve, 1, it * 2 + c, it + 1, c)

        def combine(dve, f, n, turn_no, r):
            q = ffn[f]
            dve.wait_ge(q.gathered[r], turn_no * 32)
            xt = x_sb[:, ds(n, 1), :].rearrange("p a d -> p (a d)")
            w = wts[:, ds(n, 1), :].rearrange("p a k -> p (a k)")
            dve.scalar_tensor_tensor(out=xt, in0=yg[:, r, 0, :], scalar=w[:, 0:1], in1=xt, op0=ALU.mult, op1=ALU.add)\
                .then_inc(q.half, 1)
            dve.wait_ge(q.half, n + 1)
            dve.scalar_tensor_tensor(out=xt, in0=yg[:, r, 1, :], scalar=w[:, 1:2], in1=xt, op0=ALU.mult, op1=ALU.add)\
                .then_inc(q.combined, 1)

        def norm_dve(dve, st, f):
            q = ffn[f]
            if f == 0:
                dve.wait_ge(x_loaded, 16)
            else:
                dve.wait_ge(a_x, TILES)
            for i in range(TILES // 4):
                for k in range(4):
                    ins = dve.bn_stats(st6[:, 4 * i + k, :], x_sb[:, 4 * i + k, :])
                st.link(ins)
                for k in range(4):
                    ins = dve.bn_aggr(mv[:, 4 * i + k, :], st6[:, 4 * i + k, :])
                ins.then_inc(q.stats, 1)
            for i in range(TILES // 4):
                dve.wait_ge(q.rstd, i + 1)
                for k in range(4):
                    n = 4 * i + k
                    ins = dve.tensor_scalar(out=xn_all[:, n, :], in0=x_sb[:, n, :], scalar1=mv[:, n, 0:1],
                                            scalar2=rs[:, n, 3:4], op0=ALU.subtract, op1=ALU.mult)
                ins.then_inc(q.xn, 1)

        def route_dve(dve, st, f):
            q = ffn[f]
            link = st.link
            for i in range(TILES // 4):
                dve.wait_ge(q.xhi, i + 1)
                dve.tensor_tensor(xr_l, S0[:, :], xr_h.bitcast(f32), ALU.subtract).then_inc(q.xlo, 1)
                dve.wait_ge(q.lgB, i + 1)
                ins = dve.tensor_tensor(lg[:, 4 * i:4 * i + 4, :],
                                        S1[:, 0:64].rearrange("p (k h e) -> p k h e", k=4, h=2)[:, :, 0, :],
                                        lgB[:, :, :], ALU.add)
                ins.then_inc(q.lg, 1)
            dve.wait_ge(q.lg, TILES // 4)
            te = [P, TILES, E]
            wide = lambda a: a.unsqueeze(2).to_broadcast(te)
            rev_b = rev[:, :].unsqueeze(1).to_broadcast(te)

            def first_of_max(logits, m, one):
                link(dve.tensor_reduce(m[:, :], logits, X, ALU.max))
                link(dve.tensor_tensor(r1[:, :, :], logits, wide(m[:, :]), ALU.is_equal))
                link(dve.tensor_tensor(r1[:, :, :], r1[:, :, :], rev_b, ALU.mult))
                link(dve.tensor_reduce(kk[:, :], r1[:, :, :], X, ALU.max))
                link(dve.tensor_tensor(one[:, :, :], r1[:, :, :], wide(kk[:, :]), ALU.is_equal))

            first_of_max(lg[:, :, :], m1, one1)
            link(dve.scalar_tensor_tensor(out=r2[:, :, :], in0=one1[:, :, :], scalar=-3e38, in1=lg[:, :, :],
                                          op0=ALU.mult, op1=ALU.add))
            first_of_max(r2[:, :, :], m2, one2)
            dve.tensor_tensor(e2[:, :], m2[:, :], m1[:, :], ALU.subtract).then_inc(q.gap, 1)
            dve.tensor_tensor(sel[:, :, :], one1[:, :, :], one2[:, :, :], ALU.add).then_inc(q.sel, 1)
            dve.wait_ge(q.exp2, 1)
            link(dve.tensor_scalar(out=kk[:, :], in0=e2[:, :], scalar1=1.0, scalar2=2.0, op0=ALU.add, op1=ALU.mult))
            link(dve.reciprocal(wts[:, :, 0], kk[:, :]))
            link(dve.tensor_tensor(wts[:, :, 1], wts[:, :, 0], e2[:, :], ALU.mult))
            dve.wait_ge(q.rank, 1)
            link(dve.tensor_copy(n_e[:, :], MISC[:, 128:128 + E]))
            link(dve.tensor_tensor(cmp[:, :, :], thr[:, :].unsqueeze(1).to_broadcast([P, E, TILES]),
                                   n_e[:, :].unsqueeze(2).to_broadcast([P, E, TILES]), ALU.is_lt))
            link(dve.tensor_reduce(sl_e[:, :], cmp[:, :, :], X, ALU.add))
            link(dve.tensor_tensor(mm[:, :, :], before[:, :, :], sl_e[:, :].unsqueeze(1).to_broadcast([P, E, E]), ALU.mult))
            link(dve.tensor_reduce(off[:, :], mm[:, :, :], X, ALU.add))
            dve.tensor_tensor(incl[:, :], off[:, :], sl_e[:, :], ALU.add)
            link(dve.tensor_scalar(out=offs[:, :], in0=off[:, :], scalar1=float(P), scalar2=None, op0=ALU.mult))
            link(dve.tensor_tensor(r1[:, :, :], MISC[:, 0:P].rearrange("p (n e) -> p n e", e=E),
                                   offs[:, :].unsqueeze(1).to_broadcast(te), ALU.add))
            dve.tensor_tensor(r2[:, :, :], r1[:, :, :], one1[:, :, :], ALU.mult)
            link(dve.tensor_tensor(r1[:, :, :], r1[:, :, :], one2[:, :, :], ALU.mult))
            dve.tensor_reduce(posf[:, :, 0], r2[:, :, :], X, ALU.add)
            link(dve.tensor_reduce(posf[:, :, 1], r1[:, :, :], X, ALU.add))
            dve.tensor_copy(pos[:, :, :], posf[:, :, :]).then_inc(q.pos, 1)
            link(dve.tensor_tensor(se[:, :, :], incl[0:1, :].unsqueeze(1).to_broadcast([1, SLOTS, E]),
                                   slot_j[:, :].unsqueeze(2).to_broadcast([1, SLOTS, E]), ALU.is_le))
            link(dve.tensor_reduce(sef[:, :], se[:, :, :], X, ALU.add))
            link(dve.tensor_scalar(out=sef[:, :], in0=sef[:, :], scalar1=float(E - 1), scalar2=float(WE),
                                   op0=ALU.min, op1=ALU.mult))
            dve.tensor_copy(slot_w[:, :], sef[:, :]).then_inc(q.slotw, 1)

        def slots_dve(dve, f):
            q = ffn[f]

            def turn(it, c):
                ok = lambda n: it is not None or 0 <= n < SLOTS
                j = tile_no(it, c)
                if ok(c + 1):
                    dve.wait_ge(q.xgh, j + 2)
                    dve.tensor_tensor(xg_l[:, (c + 1) % 2, :], xg_p, xg_h[:, (c + 1) % 2, :].bitcast(f32),
                                      ALU.subtract).then_inc(q.xgl, 1)
                if ok(c):
                    dve.wait_ge(q.silu, j + 1)
                    dve.wait_ge(q.up, j + 1)
                    wait(dve, q.hT, j - 1)
                    dve.tensor_tensor(h_act[:, c % 2, :], up_p[c % 2], s_act[:, c % 2, :], ALU.mult).then_inc(q.h, 1)
                if ok(c - 1):
                    dve.wait_ge(q.hTh, j)
                    dve.tensor_tensor(hT_l[:, (c - 1) % 2, :], hT_p[(c - 1) % 2], hT_h[:, (c - 1) % 2, :].bitcast(f32),
                                      ALU.subtract).then_inc(q.hTl, 1)
                if ok(c - 2):
                    dve.wait_ge(q.yB, j - 1)
                    wait(dve, q.stored[c % 2], half_no(it, c - 2) * 16)
                    dve.tensor_tensor(y_out[:, c % 2, :], y_p[:, 0:D], yB[:, :], ALU.add).then_inc(q.y, 1)
            slot_turns(dve, turn)

        def attention_dve(dve):
            def norm(it, c):
                n = tile_no(it, c)
                combine(dve, 0, n, half_no(it, c) + 1, c % 2)
                wait_apart(dve, ffn[0].combined, n + 1, const_ready)
                dve.bn_stats(st6[:, 0, :], x_sb[:, ds(n, 1), :].rearrange("p a d -> p (a d)")).then_inc(a_bn, 1)
                wait_apart(dve, a_bn, n + 1, const_ready)
                dve.bn_aggr(mv[:, 0, :], st6[:, 0, :]).then_inc(a_stats, 1)

            def xn(it, c):
                n = tile_no(it, c)
                dve.wait_ge(a_rstd, n + 1)
                dve.tensor_scalar(out=xn_t[:, c % 2, :], in0=x_sb[:, ds(n, 1), :].rearrange("p a d -> p (a d)"),
                                  scalar1=mv[:, 0, 0:1], scalar2=rs[:, 0, 3:4], op0=ALU.subtract, op1=ALU.mult)\
                    .then_inc(a_xn, 1)

            def xa_lo(it, c):
                n = tile_no(it, c)
                dve.wait_ge(a_xah, n + 1)
                dve.tensor_tensor(xa[:, 1, :], xa_f[:, :], xa[:, 0, :].bitcast(f32), ALU.subtract).then_inc(a_xal, 1)

            def qk_lo(it, c):
                n = tile_no(it, c)
                dve.wait_ge(a_qkh, n + 1)
                for k in range(2):
                    ins = dve.scalar_tensor_tensor(out=qk_hl[:, 1, k, :], in0=MISC[:, P * (k + 1):P * (k + 2)],
                                                   scalar=bqk_sb[:, k:k + 1], in1=qk_hl[:, 0, k, :].bitcast(f32),
                                                   op0=ALU.add, op1=ALU.subtract)
                ins.then_inc(a_qkl, 1)
                dve.tensor_tensor(v_st[:, c % 4, :, :, 0:HD],
                                  MISC[:, 3 * P:4 * P].rearrange("p (b c d) -> p b c d", b=NB, c=NC),
                                  bv_sb[:, :].rearrange("p (c d) -> p c d", c=NC).unsqueeze(1).to_broadcast([P, NB, NC, HD]),
                                  ALU.add).then_inc(a_v, 1)

            def row_max(it, c, u):
                n = tile_no(it, c)
                dve.wait_ge(a_s, n * 16 + u + 1)
                dve.tensor_reduce(mx[:, c % 2, u:u + 1], SB[u % 2][:, :], X, ALU.max).then_inc(a_max, 1)

            def normalise(it, c):
                n = tile_no(it, c)
                dve.wait_ge(a_nd, n * 32 + 32)
                dve.reciprocal(nd[:, 1, :], nd[:, 1, :]).then_inc(a_rec, 1)
                dve.wait_ge(a_rec, n + 1)
                dve.tensor_tensor(vals[:, :], nd[:, 0, :], nd[:, 1, :], ALU.mult).then_inc(a_vals, 1)
                dve.wait_ge(a_vh, n + 1)
                dve.tensor_tensor(vh[:, 1, :], vals[:, :], vh[:, 0, :].bitcast(f32), ALU.subtract).then_inc(a_vl, 1)

            def project(it, c):
                n = tile_no(it, c)
                dve.wait_ge(a_oB, n + 1)
                wait(dve, a_x, n)
                dve.tensor_tensor(oA[:, :], MISC[:, 0:P], oB[:, :], ALU.add).then_inc(a_oA, 1)

            def turn(it, c):
                ok = lambda n: it is not None or 0 <= n < TILES
                if ok(c + 3):
                    norm(it, c + 3)
                for u in range(16):
                    if ok(c + 2):
                        row_max(it, c + 2, u)
                    if u == 3 and ok(c + 3):
                        xn(it, c + 3)
                    if u == 7 and ok(c + 3):
                        xa_lo(it, c + 3)
                    if u == 11 and ok(c + 3):
                        qk_lo(it, c + 3)
                if ok(c - 1):
                    normalise(it, c - 1)
                    project(it, c - 1)
            for_turns(dve, turn)

        def tensor_program(pe):
            pe.wait_ge(const_ready, 1)
            for f in range(2):
                route_pe(pe, f)
                slots_pe(pe, f)
                if f == 0:
                    attention_pe(pe)

        def route_pe(pe, f):
            q = ffn[f]
            for i in range(TILES // 4):
                pe.wait_ge(q.xn, i + 1)
                wait(pe, q.xlo, i)
                for k in range(4):
                    ins = pe.transpose(S0[:, P * k:P * (k + 1)], xn_all[:, 4 * i + k, :], ident[:, :])
                ins.then_inc(q.xT, 1)
                pe.wait_ge(q.xlo, i + 1)
                if i == 0 and f == 0:
                    pe.wait_ge(small_done, 1)
                wait(pe, q.lg, i)
                for k in range(4):
                    pe.matmul(S1[:, 16 * k:16 * k + 16], xr_h[:, P * k:P * (k + 1)], w_r[:, :], start=True, stop=False)
                    ins = pe.matmul(S1[:, 16 * k:16 * k + 16], xr_l[:, P * k:P * (k + 1)], w_r[:, :], start=False, stop=True)
                ins.then_inc(q.logit, 1)
            pe.wait_ge(q.sel, 1)
            flat = sel[:, :, :].rearrange("p n e -> p (n e)")
            pe.matmul(MISC[:, 0:P], upper[:, :], flat, start=True, stop=False)
            for s in range(1, TILES):
                pe.matmul(MISC[:, E * s:P], ones_b[:, :], flat[:, 0:P - E * s], start=False, stop=(s == TILES - 1))
            for n in range(TILES):
                ins = pe.matmul(MISC[:, P:P + E], ones_b[:, :], flat[:, E * n:E * n + E], start=(n == 0), stop=(n == TILES - 1))
            ins.then_inc(q.rank, 1)

        def slots_pe(pe, f):
            q = ffn[f]
            pe.wait_ge(q.slotw, 1)
            pe.wait_ge(w_lo_done, E)
            flat = w_exp[:, :, :].rearrange("p e c -> p (e c)")

            def turn(it, c):
                ok = lambda n: it is not None or 0 <= n < SLOTS
                j = tile_no(it, c)
                if ok(c):
                    w_up = pe.value_load(slot_w[0:1, ds(j, 1)], min_val=0, max_val=WE * (E - 1))
                if ok(c - 2):
                    w_down = pe.value_load(slot_w[0:1, ds(j - 2, 1)], min_val=0, max_val=WE * (E - 1))
                if ok(c):
                    wait(pe, q.xgl, j + 1)
                if ok(c + 1):
                    pe.wait_ge(q.xg[(c + 1) % 4], quarter_no(it, c + 1) * 16 + 16)
                    pe.transpose(xg_p, xg[:, (c + 1) % 4, :], ident[:, :]).then_inc(q.xgT, 1)
                if ok(c):
                    xh, xl = xg_h[:, c % 2, :], xg_l[:, c % 2, :]
                    for dst, free, done, base in ((gate_p[c % 2], q.silu, q.gate, 0), (up_p[c % 2], q.h, q.up, 1024)):
                        wait(pe, free, j - 1)
                        pe.matmul(dst, xh, flat[:, ds(w_up + base, F)], start=True, stop=False)
                        pe.matmul(dst, xh, flat[:, ds(w_up + (base + F), F)], start=False, stop=False)
                        pe.matmul(dst, xl, flat[:, ds(w_up + base, F)], start=False, stop=True).then_inc(done, 1)
                if ok(c - 1):
                    pe.wait_ge(q.h, j)
                    wait(pe, q.hTl, j - 2)
                    r = (c - 1) % 2
                    for k in range(4):
                        ins = pe.transpose(hT_p[r][:, P * k:P * (k + 1)], h_act[:, r, P * k:P * (k + 1)], ident[:, :])
                    ins.then_inc(q.hT, 1)
                if ok(c - 2):
                    pe.wait_ge(q.hTl, j - 1)
                    wait(pe, q.y, j - 2)
                    r = c % 2
                    for k in range(4):
                        for part, src in enumerate((hT_h, hT_l)):
                            ins = pe.matmul(y_p, src[:, r, P * k:P * (k + 1)], flat[:, ds(w_down + (2048 + 256 * k), 2 * D)],
                                            start=(k == 0 and part == 0), stop=(k == 3 and part == 1))
                    ins.then_inc(q.outp, 1)
            slot_turns(pe, turn)

        def attention_pe(pe):
            def cols(t, b, c=None):
                t = t[:, b, :]
                return t if c is None else t[:, P * c:P * (c + 1)]

            def scores_for_max(it, c, u):
                n, r = tile_no(it, c), c % 4
                b, ch = u // NC, u % NC
                if u == 0:
                    pe.wait_ge(a_stacked[r], quarter_no(it, c) * 96 + 96)
                wait(pe, a_max, n * 16 + u - 1)
                pe.matmul(SB[u % 2][:, :], cols(q_st(r, KROWS), b, ch), cols(k_st(r, KROWS), b),
                          start=True, stop=True).then_inc(a_s, 1)

            def scores(it, c, k):
                n, r = tile_no(it, c), c % 4
                cp, b = k // NB, k % NB
                if k == 0:
                    pe.wait_ge(a_mrow[r], quarter_no(it, c) * 16 + 16)
                wait(pe, a_exp, n * 8 + k - 1)
                for cc in range(2):
                    ins = pe.matmul(ST[k % 2][:, 512 * cc:512 * (cc + 1)], cols(k_st(r), b, 2 * cp + cc), cols(q_st(r), b),
                                    start=True, stop=True)
                ins.then_inc(a_st, 1)

            def values(it, c, cp):
                n = tile_no(it, c)
                pe.wait_ge(a_exp, n * 8 + 4 * cp + 4)
                if cp == 0:
                    pe.wait_ge(a_v, n + 1)
                    wait(pe, a_o, n)
                for cc in range(2):
                    for b in range(NB):
                        ins = pe.matmul(PVB[32 * b:32 * b + 32, :], v_st[:, c % 4, b, 2 * cp + cc, :], prob[:, cp, b, cc, :],
                                        start=(cp == 0 and cc == 0), stop=(cp == 1 and cc == 1))
                ins.then_inc(a_pv, 1)

            def max_t(it, c):
                n = tile_no(it, c)
                pe.wait_ge(a_max, n * 16 + 16)
                pe.transpose(MISC[0:NB * NC, 0:P], mx[:, c % 2, :], ident[:, :]).then_inc(a_mT, 1)

            def x_t(it, c, after_m):
                n = tile_no(it, c)
                pe.wait_ge(a_xn, n + 1)
                if after_m:
                    pe.wait_ge(a_negm, n - 1)
                pe.transpose(MISC[:, 0:P], xn_t[:, c % 2, :], ident[:, :]).then_inc(a_xT, 1)

            def qkv(it, c):
                n = tile_no(it, c)
                pe.wait_ge(a_xal, n + 1)
                for k in range(2):
                    o = MISC[:, P * (k + 1):P * (k + 2)]
                    pe.matmul(o, w_qk[:, k, 0, :], xa[:, 0, :], start=True, stop=False)
                    pe.matmul(o, w_qk[:, k, 0, :], xa[:, 1, :], start=False, stop=False)
                    pe.matmul(o, w_qk[:, k, 1, :], xa[:, 0, :], start=False, stop=True)
                wv = w_small[:, 3 * D:4 * D].rearrange("p (i c) -> p i c", i=GC)
                for b in range(NB):
                    for g in range(GC):
                        ins = pe.matmul(MISC[32 * g:32 * g + 32, 3 * P + 32 * b:3 * P + 32 * b + 32],
                                        xa_f[:, BLK * b:BLK * (b + 1)], wv[:, g, :], start=True, stop=True)
                ins.then_inc(a_qkv, 1)

            def project(it, c):
                n = tile_no(it, c)
                pe.wait_ge(a_vl, n + 1)
                pe.matmul(MISC[:, 0:2 * P], vh[:, 0, :], w_o[:, :], start=True, stop=False)
                pe.matmul(MISC[:, 0:2 * P], vh[:, 1, :], w_o[:, :], start=False, stop=True).then_inc(a_op, 1)

            def turn(it, c):
                ok = lambda n: it is not None or 0 <= n < TILES
                n = tile_no(it, c)
                for k in range(8):
                    if ok(c):
                        scores(it, c, k)
                    if ok(c + 2):
                        scores_for_max(it, c + 2, 2 * k)
                        scores_for_max(it, c + 2, 2 * k + 1)
                    if k == 1 and ok(c - 1):
                        values(it, c - 1, 1)
                    if k == 1 and ok(c + 1):
                        if ok(c - 2) and (it is not None and c >= 2 or it is None):
                            pe.wait_ge(a_oA, n - 1)
                        elif it is not None:
                            pe.wait_ge(a_oA, n - 1)
                        wait(pe, a_v, n + 3 if ok(c + 2) else TILES)
                        max_t(it, c + 1)
                    if k == 2 and ok(c + 3):
                        if c + 3 > 0 or it is not None:
                            wait(pe, a_v, n + 3)
                        x_t(it, c + 3, ok(c + 1))
                    if k == 4 and ok(c + 3):
                        qkv(it, c + 3)
                    if k == 5 and ok(c):
                        values(it, c, 0)
                if ok(c - 1):
                    if ok(c + 3):
                        pe.wait_ge(a_v, n + 4)
                    elif ok(c + 1):
                        pe.wait_ge(a_negm, n + 2)
                    project(it, c - 1)
            for_turns(pe, turn)

        block = ctx.enter_context(nc.Block())
        block.sync(sync_program)
        block.gpsimd(gpsimd_program)
        block.scalar(scalar_program)
        block.vector(vector_program)
        block.tensor(tensor_program)


_OUT_SHAPE = (B, S, D)


def kernel(**inputs):
    import numpy as np
    import concourse.bacc as bacc
    from concourse.bass_utils import run_bass_kernel_spmd as run

    nc = bacc.Bacc("TRN2", target_bir_lowering=False, num_devices=1)
    i = {k.replace("L0_", ""): np.asarray(v) for k, v in inputs.items()}
    w = i["attn_Wqkv"].reshape(G, 3, HD, D)
    b = i["attn_bqkv"].reshape(G, 3, HD)
    wq, wk = (w[:, k].transpose(2, 1, 0).reshape(D, D) for k in (0, 1))
    wo = i["attn_Wo"].reshape(D, G, HD).transpose(2, 1, 0).reshape(D, D)
    wv = w[:, 2].reshape(NC, GC, HD, D).transpose(3, 1, 0, 2).reshape(D, D)
    bv = b[:, 2].reshape(NC, GC, HD).transpose(1, 0, 2).reshape(GC, 1, NC * HD)
    arrays = {
        "x": i["attn_x"].reshape(B * S, D),
        "w_gate_up": np.stack([i["ffn_We_gate"], i["ffn_We_in"]], axis=1),
        "w_down": i["ffn_We_out"],
        "w_att": np.concatenate([wq, wk, wo, wv, i["ffn_W_gate"]], axis=1),
        "b_qk": b[:, 0:2].transpose(2, 0, 1).reshape(D, 2),
        "b_v": np.broadcast_to(bv, (GC, BLK, NC * HD)).reshape(P, NC * HD),
        "b_o": np.broadcast_to(i["attn_bo"][None, :], (P, D)),
    }
    arrays = {f"in_{k}": np.ascontiguousarray(v) for k, v in arrays.items()}
    f32 = mybir.dt.float32
    aps = {k: nc.dram_tensor(k, v.shape, f32, kind="ExternalInput").ap() for k, v in arrays.items()}
    out = nc.dram_tensor("out", (B * S, D), f32, kind="ExternalOutput").ap()
    scratch = [nc.dram_tensor(n, s, f32, kind="Internal").ap() for n, s in (
        ("slot_x", (SLOTS * P, D)), ("slot_y", (SLOTS * P, D)), ("qk_hop", (4 * NB, P, BLK)),
        ("max_hop", (NB * NC, P)), ("att_hop", (P, S)))]
    macaron_kernel(nc, aps["in_x"], aps["in_w_gate_up"], aps["in_w_down"], aps["in_w_att"], None,
                   aps["in_b_qk"], aps["in_b_v"], aps["in_b_o"], out, *scratch)
    r = run(nc, [arrays], core_ids=[0])
    return r.results[0]["out"].reshape(_OUT_SHAPE)
```

```python
import concourse.bass as bass
from concourse import mybir
from contextlib import ExitStack

B, S, D = 4, 512, 128
HEADS, HD = 16, 8
F, E = 512, 8
P = 128
TILES = B * S // P
SLOTS = -(-(2 * TILES + E - 1) // 4) * 4
BLK = S // HEADS
NB = P // BLK
G = D // HD
GC = P // BLK
NC = G // GC
KROWS = 3 * HD
WE = 3072
EPS = 1e-5


def tile_no(it, c):
    return c if it is None else it * 4 + c


def half_no(it, c):
    return c // 2 if it is None else it * 2 + c // 2


def quarter_no(it, c):
    return c // 4 if it is None else it + c // 4


def wait(eng, sem, value):
    if isinstance(value, int) and value <= 0:
        return
    eng.wait_ge(sem, value)


def wait_apart(eng, sem, value, ready):
    value = value if isinstance(value, int) else eng.snap(value)
    eng.wait_ge(ready, 1)
    eng.wait_ge(sem, value)


def macaron_kernel(nc, x_in, w_gate_up, w_down, w_att, w_router, b_qk, b_v, b_o, out,
                   slot_x, slot_y, qk_hop, max_hop, att_hop):
    f32, f32r, bf16 = mybir.dt.float32, mybir.dt.float32r, mybir.dt.bfloat16
    i32, u32 = mybir.dt.int32, mybir.dt.uint32
    ALU = mybir.AluOpType
    ACT = mybir.ActivationFunctionType
    X = mybir.AxisListType.X
    ds = bass.ds

    ctx = ExitStack()
    with ctx:
        def sb(name, shape, dt=f32):
            return ctx.enter_context(nc.sbuf_tensor(name, shape, dt))

        def ps(name, shape):
            return ctx.enter_context(nc.psum_tensor(name, shape, f32))

        def sem(name):
            return ctx.enter_context(nc.semaphore(name))

        x_sb = sb("x_sb", [P, TILES, D])
        w_exp = sb("w_exp", [P, E, WE], f32r)
        big = sb("big", [P, 8192])
        stack = sb("stack", [P, 4096], f32r)
        xn_v = sb("xn_v", [P, TILES * D])
        qz = sb("qz", [P, NB, S], f32r)
        kz = sb("kz", [P, NB, S], f32r)
        xT_split = sb("xT_split", [P, 1536], f32r)
        w_small = sb("w_small", [P, 4 * D + E])
        w_qk = sb("w_qk", [P, 2, 2, D], f32r)
        w_o = sb("w_o", [P, 2 * D], f32r)
        w_r = sb("w_r", [P, 2 * E], f32r)
        bqk_sb = sb("bqk_sb", [P, 2])
        bv_sb = sb("bv_sb", [P, NC * HD])
        bo_sb = sb("bo_sb", [P, D])
        ident = sb("ident", [P, P])
        upper = sb("upper", [P, P], bf16)
        ones_b = sb("ones_b", [P, P], bf16)
        rev = sb("rev", [P, E])
        thr = sb("thr", [P, TILES])
        slot_j = sb("slot_j", [1, SLOTS])
        before = sb("before", [P, E, E])
        halves = sb("halves", [P, 12])
        carrier = sb("carrier", [P, 1])
        st6 = sb("st6", [P, TILES, 6])
        mv = sb("mv", [P, TILES, 2])
        rs = sb("rs", [P, TILES, 4])
        lgB = sb("lgB", [P, 4, E])
        lg = sb("lg", [P, TILES, E])
        one1 = sb("one1", [P, TILES, E])
        one2 = sb("one2", [P, TILES, E])
        sel = sb("sel", [P, TILES, E], bf16)
        m1 = sb("m1", [P, TILES])
        m2 = sb("m2", [P, TILES])
        kk = sb("kk", [P, TILES])
        e2 = sb("e2", [P, TILES])
        n_e = sb("n_e", [P, E])
        sl_e = sb("sl_e", [P, E])
        off = sb("off", [P, E])
        offs = sb("offs", [P, E])
        incl = sb("incl", [P, E])
        mm = sb("mm", [P, E, E])
        se = sb("se", [1, SLOTS, E])
        sef = sb("sef", [1, SLOTS])
        slot_w = sb("slot_w", [1, SLOTS], i32)
        posf = sb("posf", [P, TILES, 2])
        pos = sb("pos", [P, TILES, 2], u32)
        wts = sb("wts", [P, TILES, 2])
        pos_now = sb("pos_now", [P, 2, 2], u32)
        yg = sb("yg", [P, 2, 2, D])
        xn_t = sb("xn_t", [P, 2, D])
        xa_f = sb("xa_f", [P, P])
        xa = sb("xa", [P, 2, P], f32r)
        qk_hl = sb("qk_hl", [P, 2, 2, P], f32r)
        mx = sb("mx", [P, 2, NB * NC])
        neg_m = sb("neg_m", [NB * NC, P], f32r)
        o_sb = sb("o_sb", [P, S])
        nd = sb("nd", [P, 2, P])
        vals = sb("vals", [P, P])
        vh = sb("vh", [P, 2, P], f32r)
        oB = sb("oB", [P, P])
        oA = sb("oA", [P, P])

        r1, r2 = (o_sb[:, P * k:P * (k + 1)].rearrange("p (n e) -> p n e", e=E) for k in range(2))
        cmp = o_sb[:, 2 * P:3 * P].rearrange("p (e n) -> p e n", e=E)
        yB = oB
        xn_all = xn_v[:, :].rearrange("p (n d) -> p n d", n=TILES)
        v_st = xn_v[:, :].rearrange("p (r b c d) -> p r b c d", r=4, b=NB, c=NC)
        stage = big[:, 0:4 * 1536].rearrange("p (r c) -> p r c", r=4)
        zeros = big[:, 6144:8192]
        xg = big[:, 0:512].rearrange("p (r c) -> p r c", r=4)
        s_act = big[:, 512:1536].rearrange("p (r c) -> p r c", r=2)
        h_act = big[:, 1536:2560].rearrange("p (r c) -> p r c", r=2)
        y_out = big[:, 2560:2816].rearrange("p (r c) -> p r c", r=2)
        prob = big[:, :].rearrange("p (a b c s) -> p a b c s", a=2, b=NB, c=2)
        hT_h = stack[:, 0:1024].rearrange("p (r c) -> p r c", r=2)
        hT_l = stack[:, 1024:2048].rearrange("p (r c) -> p r c", r=2)
        xg_h = xT_split[:, 0:256].rearrange("p (r c) -> p r c", r=2)
        xg_l = xT_split[:, 256:512].rearrange("p (r c) -> p r c", r=2)
        xr_h = xT_split[:, 512:1024]
        xr_l = xT_split[:, 1024:1536]
        def q_st(r):
            return stack[:, 1024 * r:1024 * r + S]

        def k_st(r):
            return stack[:, 1024 * r + S:1024 * r + 2 * S]

        S0 = ps("S0", [P, 512])
        S1 = ps("S1", [P, 512])
        ST0 = ps("ST0", [P, 1024])
        ST1 = ps("ST1", [P, 1024])
        PVB = ps("PVB", [P, 512])
        MISC = ps("MISC", [P, 512])
        SB = [S0, S1]
        ST = [ST0, ST1]
        gate_p = [S0[:, :], S1[:, :]]
        up_p = [ST0[:, 0:512], ST0[:, 512:1024]]
        hT_p = [ST1[:, 0:512], ST1[:, 512:1024]]
        xg_p = PVB[:, 0:P]
        y_p = MISC[:, 0:2 * D]

        x_loaded, small_loaded, w_raw = sem("x_loaded"), sem("small_loaded"), [sem(f"w_raw{i}") for i in range(4)]
        zero_ready, zeroed, hop_init = sem("zero_ready"), sem("zeroed"), sem("hop_init")
        a_qz, a_kz, v_ones = [sem(f"a_qz{b}") for b in range(NB)], sem("a_kz"), sem("v_ones")
        const_ready, pool_step = sem("const_ready"), sem("pool_step")
        w_hi_done, w_lo_done = sem("w_hi_done"), sem("w_lo_done")
        small_hi, small_done = sem("small_hi"), sem("small_done")
        dve_step = sem("dve_step")

        class Phase:
            def __init__(self, f):
                self.stats, self.rstd, self.xn, self.xT = (
                    sem(f"stats_{f}"), sem(f"rstd_{f}"), sem(f"xn_{f}"), sem(f"xT_{f}"))
                self.xhi, self.xlo, self.logit, self.lgB = (
                    sem(f"xhi_{f}"), sem(f"xlo_{f}"), sem(f"logit_{f}"), sem(f"lgB_{f}"))
                self.lg, self.gap, self.exp2, self.sel = (
                    sem(f"lg_{f}"), sem(f"gap_{f}"), sem(f"exp2_{f}"), sem(f"sel_{f}"))
                self.rank, self.pos, self.slotw, self.sent = (
                    sem(f"rank_{f}"), sem(f"pos_{f}"), sem(f"slotw_{f}"), sem(f"sent_{f}"))
                self.xgT, self.xgh, self.xgl, self.gate = (
                    sem(f"xgT_{f}"), sem(f"xgh_{f}"), sem(f"xgl_{f}"), sem(f"gate_{f}"))
                self.up, self.silu, self.h, self.hT = (
                    sem(f"up_{f}"), sem(f"silu_{f}"), sem(f"h_{f}"), sem(f"hT_{f}"))
                self.hTh, self.hTl, self.outp, self.yB = (
                    sem(f"hTh_{f}"), sem(f"hTl_{f}"), sem(f"outp_{f}"), sem(f"yB_{f}"))
                self.y, self.half, self.combined, self.pos_now = (
                    sem(f"y_{f}"), sem(f"half_{f}"), sem(f"combined_{f}"), sem(f"pos_now_{f}"))
                self.xg = [sem(f"xg{r}_{f}") for r in range(4)]
                self.stored = [sem(f"stored{r}_{f}") for r in range(2)]
                self.gathered = [sem(f"gathered{r}_{f}") for r in range(2)]

        ffn = [Phase(0), Phase(1)]
        a_stats, a_rstd, a_xn, a_xT, a_xah, a_xal = map(sem, (
            "a_stats", "a_rstd", "a_xn", "a_xT", "a_xah", "a_xal"))
        a_qk, a_qkh, a_qkl, a_vp, a_v = map(sem, ("a_qk", "a_qkh", "a_qkl", "a_vp", "a_v"))
        a_hop = sem("a_hop")
        a_stacked = [sem(f"a_stacked{r}") for r in range(4)]
        a_s, a_max = sem("a_s"), sem("a_max")
        a_mT, a_negm, a_mhop = sem("a_mT"), sem("a_negm"), sem("a_mhop")
        a_mrow = [sem(f"a_mrow{r}") for r in range(4)]
        a_st, a_exp, a_pv, a_o = sem("a_st"), sem("a_exp"), sem("a_pv"), sem("a_o")
        a_ohop, a_nd = sem("a_ohop"), sem("a_nd")
        a_vals, a_vh, a_vl, a_op, a_oB, a_oA, a_x = map(sem, (
            "a_vals", "a_vh", "a_vl", "a_op", "a_oB", "a_oA", "a_x"))
        stored_out = sem("stored_out")
        a_pool_step, a_ob, a_bn, a_rec = map(sem, ("a_pool_step", "a_ob", "a_bn", "a_rec"))

        class Steps:
            def __init__(self, eng, s):
                self.eng, self.s, self.n = eng, s, 0

            def link(self, ins):
                self.n += 1
                ins.then_inc(self.s, 1)
                self.eng.wait_ge(self.s, self.n)

        def sync_program(sp):
            sp.dma_start(x_sb[:, :, :], x_in.rearrange("(n p) d -> p n d", p=P)).then_inc(x_loaded, 16)
            sp.dma_start(w_small[:, :], w_att).then_inc(small_loaded, 16)
            sp.dma_start(bqk_sb[:, :], b_qk).then_inc(small_loaded, 16)
            sp.dma_start(bv_sb[:, :], b_v).then_inc(small_loaded, 16)
            sp.dma_start(bo_sb[:, :], b_o).then_inc(small_loaded, 16)
            for e in range(E):
                r = e % 4
                wait(sp, w_lo_done, e - 3)
                sp.dma_start(stage[:, r, 0:1024].rearrange("p (k f) -> p k f", k=2),
                             w_gate_up[e:e + 1].rearrange("e k p f -> p (e k) f")).then_inc(w_raw[r], 16)
                sp.dma_start(stage[:, r, 1024:1536].rearrange("p (c d) -> p c d", c=4),
                             w_down[e:e + 1].rearrange("e (c p) d -> p (e c) d", p=P)).then_inc(w_raw[r], 16)

            sp.wait_ge(pool_step, 3)
            for r in range(2):
                sp.dma_start(qk_hop[r].rearrange("k p s -> p k s"),
                             stack[:, 0:2 * S].rearrange("p (k s) -> p k s", k=2).bitcast(f32)).then_inc(hop_init, 16)
            sp.wait_ge(hop_init, 32)
            sp.wait_ge(zero_ready, 1)
            for a in range(0, SLOTS, 8):
                sp.dma_start(slot_x[a * P:(a + 8) * P, :].rearrange("(n p) d -> p n d", p=P),
                             zeros[:, 0:1024].rearrange("p (n d) -> p n d", d=D)).then_inc(zeroed, 16)
            slots_sp(sp, 0)
            attention_sp(sp)
            slots_sp(sp, 1)
            q = ffn[1]
            with sp.Fori(0, TILES // 4) as it:
                sp.wait_ge(q.combined, it * 4 + 4)
                sp.dma_start(out.rearrange("(n p) d -> p n d", p=P)[:, ds(it * 4, 4), :],
                             x_sb[:, ds(it * 4, 4), :]).then_inc(stored_out, 16)
            sp.wait_ge(stored_out, 16 * (TILES // 4))

        def slots_sp(sp, f):
            q = ffn[f]

            def load(it, c):
                j, r = tile_no(it, c), c % 4
                wait(sp, q.xgT, j - 3 if not isinstance(j, int) or j >= 4 else 0)
                sp.dma_start(xg[:, r, :], slot_x[ds(j * P, P), :]).then_inc(q.xg[r], 16)

            def store(it, c):
                j, r = tile_no(it, c), c % 2
                sp.wait_ge(q.y, j + 1)
                sp.dma_start(slot_y[ds(j * P, P), :], y_out[:, r, :]).then_inc(q.stored[r], 16)

            sp.wait_ge(q.sent, 16 * 2 * TILES)
            if f == 0:
                sp.wait_ge(w_lo_done, E)
            else:
                sp.wait_ge(a_pv, 2 * TILES)
            for c in range(4):
                load(None, c)
            with sp.Fori(0, SLOTS // 4 - 1) as it:
                for c in range(4):
                    load(it, c + 4)
                    store(it, c)
            for c in range(4):
                store(None, SLOTS - 4 + c)
            if f == 0:
                pass

        def attention_sp(sp):
            def qk_write(it, c):
                n = tile_no(it, c)
                sp.wait_ge(a_qkl, n + 1)
                rows = qk_hop[c % 2].rearrange("k (b r) (g t) -> k (r g) b t", b=NB, g=G)
                for k, part, h in ((0, 0, 0), (0, 1, 1), (0, 2, 0), (1, 0, 0), (1, 1, 0), (1, 2, 1)):
                    sp.dma_start(rows[k, P * part:P * (part + 1)],
                                 qk_hl[:, k, h, :].rearrange("p (b t) -> p b t", t=BLK).bitcast(f32)).then_inc(a_hop, 16)

            def qk_read(it, c):
                n, r = tile_no(it, c), c % 4
                sp.wait_ge(a_hop, n * 96 + 96)
                wait(sp, a_st, n * 8 - 24 if not isinstance(n, int) or n >= 4 else 0)
                sp.dma_start(stack[:, 1024 * r:1024 * (r + 1)].rearrange("p (k s) -> p k s", k=2).bitcast(f32),
                             qk_hop[c % 2].rearrange("k p s -> p k s")).then_inc(a_stacked[r], 16)

            def fill_qz(it, c, b):
                n = tile_no(it, c)
                wait(sp, a_s, n * 16 + NC * b - 12)
                sp.dma_start(qz[32 * b:32 * b + KROWS, b, :].bitcast(f32), qk_hop[c % 2, 0, 32 * b:32 * b + KROWS, :])\
                    .then_inc(a_qz[b], 16)

            def max_write(it, c):
                sp.wait_ge(a_negm, tile_no(it, c) + 1)
                sp.dma_start(max_hop, neg_m[:, :].bitcast(f32)).then_inc(a_mhop, 16)

            def max_read(it, c):
                n, r = tile_no(it, c), c % 4
                sp.wait_ge(a_mhop, n * 16 + 16)
                for b in range(NB):
                    row = 32 * b + KROWS
                    sp.dma_start(q_st(r)[row:row + 1, :].bitcast(f32),
                                 max_hop[NC * b:NC * (b + 1), :].rearrange("(o a) s -> o (a s)", o=1))\
                        .then_inc(a_mrow[r], 16)

            def out_hop(it, c):
                n = tile_no(it, c)
                sp.wait_ge(a_o, n + 1)
                sp.dma_start(att_hop, o_sb[:, :]).then_inc(a_ohop, 16)
                sp.wait_ge(a_ohop, n * 16 + 16)
                wait(sp, a_vals, n)
                src = att_hop.rearrange("(b k d) (g t) -> k (d g) b t", b=NB, k=4, g=G)
                for k in range(2):
                    sp.dma_start(nd[:, k, :].rearrange("p (b t) -> p b t", b=NB), src[k]).then_inc(a_nd, 16)

            def turn(it, c):
                ok = lambda n: it is not None or 0 <= n < TILES
                if ok(c + 2):
                    fill_qz(it, c + 2, 3)
                if ok(c + 3):
                    qk_write(it, c + 3)
                if ok(c + 1):
                    max_write(it, c + 1)
                if ok(c + 1):
                    max_read(it, c + 1)
                if ok(c + 3):
                    qk_read(it, c + 3)
                if ok(c - 1):
                    out_hop(it, c - 1)
                if ok(c + 3):
                    for b in range(3):
                        fill_qz(it, c + 3, b)

            for_turns(sp, turn)

        def for_turns(eng, turn):
            for c in range(-4, 2):
                turn(None, c)
            with eng.Fori(0, 2) as it:
                for c in range(2, 6):
                    turn(it, c)
            for c in range(10, TILES + 2):
                turn(None, c)

        def gpsimd_program(pool):
            st = Steps(pool, pool_step)
            pool.memset(zeros, 0.0).then_inc(zero_ready, 1)
            st.link(pool.memset(ident[:, :], 0.0))
            pool.memset(ones_b[:, :], 1.0)
            st.link(pool.memset(before[:, :, :], 1.0))
            for k, value in enumerate((-0.5, 1.5, EPS)):
                pool.memset(halves[:, 4 * k:4 * k + 4], value)
            pool.memset(qz[:, :, :].bitcast(f32), 0.0)
            pool.memset(kz[:, :, :].bitcast(f32), 0.0)
            pool.memset(stack[:, 0:S].bitcast(f32), 0.0)
            st.link(pool.memset(stack[:, S:2 * S].bitcast(f32), 1.0))
            pool.affine_select(out=ident[:, :], in_=ident[:, :], compare_op=ALU.not_equal, fill=1.0,
                               base=0, pattern=[[-1, P]], channel_multiplier=1)
            pool.affine_select(out=upper[:, :], in_=ones_b[:, :], compare_op=ALU.is_gt, fill=0.0,
                               base=0, pattern=[[1, P]], channel_multiplier=-1)
            pool.affine_select(out=before[:, :, :], in_=before[:, :, :], compare_op=ALU.is_gt, fill=0.0,
                               base=0, pattern=[[1, E], [-1, E]], channel_multiplier=0)
            pool.iota(rev[:, :], pattern=[[-1, E]], base=E, channel_multiplier=0,
                      allow_small_or_imprecise_dtypes=True)
            pool.iota(thr[:, :], pattern=[[P, TILES]], base=0, channel_multiplier=0,
                      allow_small_or_imprecise_dtypes=True)
            pool.iota(slot_j[:, :], pattern=[[1, SLOTS]], base=0, channel_multiplier=0,
                      allow_small_or_imprecise_dtypes=True).then_inc(const_ready, 1)
            pool.wait_ge(const_ready, 1)

            for f in range(2):
                route_pool(pool, st, f)
                if f == 0:
                    pool.wait_ge(zeroed, 16 * (SLOTS // 8))
                scatter_pool(pool, f)
                if f == 0:
                    attention_pool(pool, st)
            q = ffn[1]
            for r in range(2):
                pool.wait_ge(q.stored[r], 16 * SLOTS // 2)
            for c in range(2):
                gather(pool, 1, c, 1, c)
            with pool.Fori(1, TILES // 2) as it:
                for c in range(2):
                    gather(pool, 1, it * 2 + c, it + 1, c)

        def rstd_chain(pool, link, m, r):
            c = [halves[:, k * 4:k * 4 + m.shape[1]] for k in range(3)]
            link(pool.tensor_tensor(out=r[:, :, 1], in0=m[:, :, 1], in1=c[2], op=ALU.add))
            link(pool.tensor_tensor(out=r[:, :, 0], in0=r[:, :, 1], in1=c[0], op=ALU.pow))
            link(pool.tensor_tensor(out=r[:, :, 2], in0=r[:, :, 0], in1=r[:, :, 0], op=ALU.mult))
            link(pool.tensor_tensor(out=r[:, :, 2], in0=r[:, :, 2], in1=r[:, :, 1], op=ALU.mult))
            link(pool.tensor_tensor(out=r[:, :, 2], in0=r[:, :, 2], in1=c[0], op=ALU.mult))
            link(pool.tensor_tensor(out=r[:, :, 2], in0=r[:, :, 2], in1=c[1], op=ALU.add))
            return pool.tensor_tensor(out=r[:, :, 3], in0=r[:, :, 2], in1=r[:, :, 0], op=ALU.mult)

        def route_pool(pool, st, f):
            q = ffn[f]
            for i in range(TILES // 4):
                pool.wait_ge(q.stats, i + 1)
                rstd_chain(pool, st.link, mv[:, 4 * i:4 * i + 4, :], rs[:, 4 * i:4 * i + 4, :]).then_inc(q.rstd, 1)

        def scatter_pool(pool, f):
            q = ffn[f]
            pool.wait_ge(q.pos, 1)
            for n in range(TILES):
                for k in range(2):
                    pool.indirect_dma_start(slot_x, bass.IndirectOffsetOnAxis(ap=pos[:, n, k:k + 1], axis=0),
                                            xn_all[:, n, :], None).then_inc(q.sent, 16)

        def gather(pool, f, n, turn_no, r):
            q = ffn[f]
            wait(pool, q.combined, n - 1)
            pool.tensor_copy(out=pos_now[:, r, :], in_=pos[:, ds(n, 1), :].rearrange("p a k -> p (a k)"))\
                .then_inc(q.pos_now, 1)
            pool.wait_ge(q.pos_now, n + 1)
            pool.tensor_tensor(out=carrier[:, :], in0=halves[:, 0:1], in1=halves[:, 0:1], op=ALU.add)
            for k in range(2):
                pool.indirect_dma_start(yg[:, r, k, :], None, slot_y,
                                        bass.IndirectOffsetOnAxis(ap=pos_now[:, r, k:k + 1], axis=0))\
                    .then_inc(q.gathered[r], 16)

        def attention_pool(pool, st):
            q = ffn[0]
            pool.wait_ge(q.sent, 16 * 2 * TILES)
            pool.memset(v_st[:, :, :, :, :], 1.0).then_inc(v_ones, 1)
            for r in range(2):
                pool.wait_ge(q.stored[r], 16 * SLOTS // 2)

            def rest(it, c):
                n = tile_no(it, c)
                pool.wait_ge(a_stats, n + 1)
                steps = [0]

                def link(ins):
                    steps[0] += 1
                    ins.then_inc(a_pool_step, 1)
                    pool.wait_ge(a_pool_step, n * 6 + steps[0])
                rstd_chain(pool, link, mv[:, 0:1, :], rs[:, 0:1, :]).then_inc(a_rstd, 1)

            def normalise(it, c):
                n = tile_no(it, c)
                pool.wait_ge(a_rec, n + 1)
                wait(pool, a_vl, n)
                pool.tensor_tensor(out=vals[:, :], in0=nd[:, 0, :], in1=nd[:, 1, :], op=ALU.mult).then_inc(a_vals, 1)

            def residual(it, c):
                n = tile_no(it, c)
                pool.wait_ge(a_oA, n + 1)
                xt = x_sb[:, ds(n, 1), :].rearrange("p a d -> p (a d)")
                pool.tensor_tensor(out=oA[:, :], in0=oA[:, :], in1=bo_sb[:, :], op=ALU.add).then_inc(a_ob, 1)
                pool.wait_ge(a_ob, n + 1)
                pool.tensor_tensor(out=xt, in0=xt, in1=oA[:, :], op=ALU.add).then_inc(a_x, 1)

            def turn(it, c):
                ok = lambda n: it is not None or 0 <= n < TILES
                if ok(c - 2):
                    normalise(it, c - 2)
                if ok(c + 4):
                    rest(it, c + 4)
                if ok(c - 2):
                    residual(it, c - 2)
                if ok(c + 5):
                    gather(pool, 0, tile_no(it, c + 5), half_no(it, c + 5) + 1, (c + 5) % 2)
            gather(pool, 0, 0, 1, 0)
            for_turns(pool, turn)

        def scalar_program(act):
            act.wait_ge(small_loaded, 64)
            act.activation(w_qk[:, :, 0, :], w_small[:, 0:2 * D].rearrange("p (k d) -> p k d", k=2), ACT.Copy).then_inc(small_hi, 1)
            act.activation(w_o[:, 0:D], w_small[:, 2 * D:3 * D], ACT.Copy).then_inc(small_hi, 1)
            act.activation(w_r[:, 0:E], w_small[:, 4 * D:4 * D + E], ACT.Copy).then_inc(small_hi, 1)
            for f in range(2):
                route_act(act, f)
                if f == 0:
                    with act.Fori(0, E // 4) as it:
                        for r in range(4):
                            act.wait_ge(w_raw[r], it * 32 + 32)
                            we = w_exp[:, ds(it * 4 + r, 1), :].rearrange("p a c -> p (a c)")
                            act.activation(we[:, 0:2048].rearrange("p (k h f) -> p k h f", k=2, h=2)[:, :, 0, :],
                                           stage[:, r, 0:1024].rearrange("p (k f) -> p k f", k=2), ACT.Copy)
                            act.activation(we[:, 2048:3072].rearrange("p (c h d) -> p c h d", c=4, h=2)[:, :, 0, :],
                                           stage[:, r, 1024:1536].rearrange("p (c d) -> p c d", c=4), ACT.Copy).then_inc(w_hi_done, 1)
                slots_act(act, f)
                if f == 0:
                    attention_act(act)

        def route_act(act, f):
            q = ffn[f]
            for i in range(TILES // 4):
                act.wait_ge(q.xT, i + 1)
                wait(act, q.logit, i)
                act.activation(xr_h, S0[:, :], ACT.Copy).then_inc(q.xhi, 1)
                act.wait_ge(q.logit, i + 1)
                wait(act, q.lg, i)
                act.activation(lgB[:, :, :], S1[:, 0:64].rearrange("p (k h e) -> p k h e", k=4, h=2)[:, :, 1, :],
                               ACT.Copy).then_inc(q.lgB, 1)
            act.wait_ge(q.gap, 1)
            act.activation(e2[:, :], e2[:, :], ACT.Exp).then_inc(q.exp2, 1)

        def slots_act(act, f):
            q = ffn[f]

            def turn(it, c):
                ok = lambda n: it is not None or 0 <= n < SLOTS
                j = tile_no(it, c)
                if ok(c + 1):
                    act.wait_ge(q.xgT, j + 2)
                    wait(act, q.up, j)
                    act.activation(xg_h[:, (c + 1) % 2, :], xg_p, ACT.Copy).then_inc(q.xgh, 1)
                if ok(c):
                    act.wait_ge(q.gate, j + 1)
                    wait(act, q.h, j - 1)
                    act.activation(s_act[:, c % 2, :], gate_p[c % 2], ACT.Silu).then_inc(q.silu, 1)
                if ok(c - 1):
                    act.wait_ge(q.hT, j)
                    wait(act, q.outp, j - 2)
                    act.activation(hT_h[:, (c - 1) % 2, :], hT_p[(c - 1) % 2], ACT.Copy).then_inc(q.hTh, 1)
                if ok(c - 2):
                    act.wait_ge(q.outp, j - 1)
                    wait(act, q.y, j - 2)
                    act.activation(yB[:, :], y_p[:, D:2 * D], ACT.Copy).then_inc(q.yB, 1)
            slot_turns(act, turn)

        def slot_turns(eng, turn):
            for c in range(-1, 4):
                turn(None, c)
            with eng.Fori(0, SLOTS // 4 - 2) as it:
                for c in range(4, 8):
                    turn(it, c)
            for c in range(SLOTS - 4, SLOTS + 2):
                turn(None, c)

        def attention_act(act):
            def exps(it, c, k):
                n, cp, b = tile_no(it, c), k // NB, k % NB
                act.wait_ge(a_st, n * 8 + k + 1)
                wait(act, a_pv, n * 2 + cp - 1)
                act.activation(prob[:, cp, b, :, :].rearrange("p c s -> p (c s)"), ST[k % 2][:, :], ACT.Exp,
                               scale=HD ** -0.5).then_inc(a_exp, 1)

            def fill_kz(it, c, b):
                n, r = tile_no(it, c), c % 4
                act.wait_ge(a_stacked[r], quarter_no(it, c) * 16 + 16)
                wait(act, a_st, n * 8 + b - 3)
                rows = slice(32 * b, 32 * b + KROWS + 1)
                act.activation(kz[rows, b, :], k_st(r)[rows, :].bitcast(f32), ACT.Copy).then_inc(a_kz, 1)

            def negm(it, c):
                n = tile_no(it, c)
                act.wait_ge(a_mT, n + 1)
                wait(act, a_mhop, n * 16)
                act.activation(neg_m[:, :], MISC[0:NB * NC, 0:P], ACT.Copy, scale=-1.0).then_inc(a_negm, 1)

            def xa_evac(it, c):
                n = tile_no(it, c)
                act.wait_ge(a_xT, n + 1)
                wait(act, a_vp, n)
                act.activation(xa_f[:, :], MISC[:, 0:P], ACT.Copy)
                act.activation(xa[:, 0, :], MISC[:, 0:P], ACT.Copy).then_inc(a_xah, 1)

            def qk_evac(it, c):
                n = tile_no(it, c)
                act.wait_ge(a_qk, n + 1)
                wait(act, a_hop, n * 96)
                for k in range(2):
                    ins = act.activation(qk_hl[:, k, 0, :], MISC[:, P * (k + 1):P * (k + 2)], ACT.Identity,
                                         bias=bqk_sb[:, k:k + 1])
                ins.then_inc(a_qkh, 1)

            def o_evac(it, c):
                n = tile_no(it, c)
                act.wait_ge(a_pv, n * 2 + 2)
                wait(act, a_ohop, n * 16)
                act.activation(o_sb[:, :], PVB[:, :], ACT.Copy).then_inc(a_o, 1)

            def vals_hi(it, c):
                n = tile_no(it, c)
                act.wait_ge(a_vals, n + 1)
                wait(act, a_op, n)
                act.activation(vh[:, 0, :], vals[:, :], ACT.Copy).then_inc(a_vh, 1)

            def op_evac(it, c):
                n = tile_no(it, c)
                act.wait_ge(a_op, n + 1)
                wait(act, a_oA, n)
                act.activation(oB[:, :], MISC[:, 2 * P:3 * P], ACT.Copy).then_inc(a_oB, 1)

            def turn(it, c):
                ok = lambda n: it is not None or 0 <= n < TILES
                for k in range(8):
                    if k == 0 and ok(c + 3):
                        qk_evac(it, c + 3)
                    if ok(c):
                        exps(it, c, k)
                    if k >= NB and ok(c + 1):
                        fill_kz(it, c + 1, k - NB)
                    if k == 1 and ok(c + 1):
                        negm(it, c + 1)
                    if k == 2 and ok(c - 2):
                        vals_hi(it, c - 2)
                    if k == 2 and ok(c - 1):
                        o_evac(it, c - 1)
                    if k == 4 and ok(c - 2):
                        op_evac(it, c - 2)
                    if k == 6 and ok(c + 4):
                        xa_evac(it, c + 4)
            for_turns(act, turn)

        def vector_program(dve):
            st = Steps(dve, dve_step)
            dve.wait_ge(const_ready, 1)
            for f in range(2):
                norm_dve(dve, st, f)
                if f == 0:
                    dve.wait_ge(small_hi, 3)
                    dve.tensor_tensor(w_qk[:, :, 1, :], w_small[:, 0:2 * D].rearrange("p (k d) -> p k d", k=2),
                                      w_qk[:, :, 0, :].bitcast(f32), ALU.subtract)
                    dve.tensor_tensor(w_o[:, D:2 * D], w_small[:, 2 * D:3 * D], w_o[:, 0:D].bitcast(f32), ALU.subtract)
                    dve.tensor_tensor(w_r[:, E:2 * E], w_small[:, 4 * D:4 * D + E], w_r[:, 0:E].bitcast(f32),
                                      ALU.subtract).then_inc(small_done, 1)
                route_dve(dve, st, f)
                if f == 0:
                    with dve.Fori(0, E // 4) as it:
                        for r in range(4):
                            dve.wait_ge(w_hi_done, it * 4 + r + 1)
                            we = w_exp[:, ds(it * 4 + r, 1), :].rearrange("p a c -> p (a c)")
                            gu = we[:, 0:2048].rearrange("p (k h f) -> p k h f", k=2, h=2)
                            dn = we[:, 2048:3072].rearrange("p (c h d) -> p c h d", c=4, h=2)
                            dve.tensor_tensor(gu[:, :, 1, :], stage[:, r, 0:1024].rearrange("p (k f) -> p k f", k=2),
                                              gu[:, :, 0, :].bitcast(f32), ALU.subtract)
                            dve.tensor_tensor(dn[:, :, 1, :], stage[:, r, 1024:1536].rearrange("p (c d) -> p c d", c=4),
                                              dn[:, :, 0, :].bitcast(f32), ALU.subtract).then_inc(w_lo_done, 1)
                slots_dve(dve, f)
                if f == 0:
                    attention_dve(dve)
            q = ffn[1]
            with dve.Fori(0, TILES // 2) as it:
                for c in range(2):
                    combine(dve, 1, it * 2 + c, it + 1, c)

        def combine(dve, f, n, turn_no, r):
            q = ffn[f]
            dve.wait_ge(q.gathered[r], turn_no * 32)
            xt = x_sb[:, ds(n, 1), :].rearrange("p a d -> p (a d)")
            w = wts[:, ds(n, 1), :].rearrange("p a k -> p (a k)")
            dve.scalar_tensor_tensor(out=xt, in0=yg[:, r, 0, :], scalar=w[:, 0:1], in1=xt, op0=ALU.mult, op1=ALU.add)\
                .then_inc(q.half, 1)
            dve.wait_ge(q.half, n + 1)
            dve.scalar_tensor_tensor(out=xt, in0=yg[:, r, 1, :], scalar=w[:, 1:2], in1=xt, op0=ALU.mult, op1=ALU.add)\
                .then_inc(q.combined, 1)

        def norm_dve(dve, st, f):
            q = ffn[f]
            if f == 0:
                dve.wait_ge(x_loaded, 16)
            else:
                dve.wait_ge(a_x, TILES)
            for i in range(TILES // 4):
                for k in range(4):
                    ins = dve.bn_stats(st6[:, 4 * i + k, :], x_sb[:, 4 * i + k, :])
                st.link(ins)
                for k in range(4):
                    ins = dve.bn_aggr(mv[:, 4 * i + k, :], st6[:, 4 * i + k, :])
                ins.then_inc(q.stats, 1)
            for i in range(TILES // 4):
                dve.wait_ge(q.rstd, i + 1)
                for k in range(4):
                    n = 4 * i + k
                    ins = dve.tensor_scalar(out=xn_all[:, n, :], in0=x_sb[:, n, :], scalar1=mv[:, n, 0:1],
                                            scalar2=rs[:, n, 3:4], op0=ALU.subtract, op1=ALU.mult)
                ins.then_inc(q.xn, 1)

        def route_dve(dve, st, f):
            q = ffn[f]
            link = st.link
            for i in range(TILES // 4):
                dve.wait_ge(q.xhi, i + 1)
                dve.tensor_tensor(xr_l, S0[:, :], xr_h.bitcast(f32), ALU.subtract).then_inc(q.xlo, 1)
                dve.wait_ge(q.lgB, i + 1)
                ins = dve.tensor_tensor(lg[:, 4 * i:4 * i + 4, :],
                                        S1[:, 0:64].rearrange("p (k h e) -> p k h e", k=4, h=2)[:, :, 0, :],
                                        lgB[:, :, :], ALU.add)
                ins.then_inc(q.lg, 1)
            dve.wait_ge(q.lg, TILES // 4)
            te = [P, TILES, E]
            wide = lambda a: a.unsqueeze(2).to_broadcast(te)
            rev_b = rev[:, :].unsqueeze(1).to_broadcast(te)

            def first_of_max(logits, m, one):
                link(dve.tensor_reduce(m[:, :], logits, X, ALU.max))
                link(dve.tensor_tensor(r1[:, :, :], logits, wide(m[:, :]), ALU.is_equal))
                link(dve.tensor_tensor(r1[:, :, :], r1[:, :, :], rev_b, ALU.mult))
                link(dve.tensor_reduce(kk[:, :], r1[:, :, :], X, ALU.max))
                link(dve.tensor_tensor(one[:, :, :], r1[:, :, :], wide(kk[:, :]), ALU.is_equal))

            first_of_max(lg[:, :, :], m1, one1)
            link(dve.scalar_tensor_tensor(out=r2[:, :, :], in0=one1[:, :, :], scalar=-3e38, in1=lg[:, :, :],
                                          op0=ALU.mult, op1=ALU.add))
            first_of_max(r2[:, :, :], m2, one2)
            dve.tensor_tensor(e2[:, :], m2[:, :], m1[:, :], ALU.subtract).then_inc(q.gap, 1)
            dve.tensor_tensor(sel[:, :, :], one1[:, :, :], one2[:, :, :], ALU.add).then_inc(q.sel, 1)
            dve.wait_ge(q.exp2, 1)
            link(dve.tensor_scalar(out=kk[:, :], in0=e2[:, :], scalar1=1.0, scalar2=2.0, op0=ALU.add, op1=ALU.mult))
            link(dve.reciprocal(wts[:, :, 0], kk[:, :]))
            link(dve.tensor_tensor(wts[:, :, 1], wts[:, :, 0], e2[:, :], ALU.mult))
            dve.wait_ge(q.rank, 1)
            link(dve.tensor_copy(n_e[:, :], MISC[:, 128:128 + E]))
            link(dve.tensor_tensor(cmp[:, :, :], thr[:, :].unsqueeze(1).to_broadcast([P, E, TILES]),
                                   n_e[:, :].unsqueeze(2).to_broadcast([P, E, TILES]), ALU.is_lt))
            link(dve.tensor_reduce(sl_e[:, :], cmp[:, :, :], X, ALU.add))
            link(dve.tensor_tensor(mm[:, :, :], before[:, :, :], sl_e[:, :].unsqueeze(1).to_broadcast([P, E, E]), ALU.mult))
            link(dve.tensor_reduce(off[:, :], mm[:, :, :], X, ALU.add))
            dve.tensor_tensor(incl[:, :], off[:, :], sl_e[:, :], ALU.add)
            link(dve.tensor_scalar(out=offs[:, :], in0=off[:, :], scalar1=float(P), scalar2=None, op0=ALU.mult))
            link(dve.tensor_tensor(r1[:, :, :], MISC[:, 0:P].rearrange("p (n e) -> p n e", e=E),
                                   offs[:, :].unsqueeze(1).to_broadcast(te), ALU.add))
            dve.tensor_tensor(r2[:, :, :], r1[:, :, :], one1[:, :, :], ALU.mult)
            link(dve.tensor_tensor(r1[:, :, :], r1[:, :, :], one2[:, :, :], ALU.mult))
            dve.tensor_reduce(posf[:, :, 0], r2[:, :, :], X, ALU.add)
            link(dve.tensor_reduce(posf[:, :, 1], r1[:, :, :], X, ALU.add))
            dve.tensor_copy(pos[:, :, :], posf[:, :, :]).then_inc(q.pos, 1)
            link(dve.tensor_tensor(se[:, :, :], incl[0:1, :].unsqueeze(1).to_broadcast([1, SLOTS, E]),
                                   slot_j[:, :].unsqueeze(2).to_broadcast([1, SLOTS, E]), ALU.is_le))
            link(dve.tensor_reduce(sef[:, :], se[:, :, :], X, ALU.add))
            link(dve.tensor_scalar(out=sef[:, :], in0=sef[:, :], scalar1=float(E - 1), scalar2=float(WE),
                                   op0=ALU.min, op1=ALU.mult))
            dve.tensor_copy(slot_w[:, :], sef[:, :]).then_inc(q.slotw, 1)

        def slots_dve(dve, f):
            q = ffn[f]

            def turn(it, c):
                ok = lambda n: it is not None or 0 <= n < SLOTS
                j = tile_no(it, c)
                if ok(c + 1):
                    dve.wait_ge(q.xgh, j + 2)
                    dve.tensor_tensor(xg_l[:, (c + 1) % 2, :], xg_p, xg_h[:, (c + 1) % 2, :].bitcast(f32),
                                      ALU.subtract).then_inc(q.xgl, 1)
                if ok(c):
                    dve.wait_ge(q.silu, j + 1)
                    dve.wait_ge(q.up, j + 1)
                    wait(dve, q.hT, j - 1)
                    dve.tensor_tensor(h_act[:, c % 2, :], up_p[c % 2], s_act[:, c % 2, :], ALU.mult).then_inc(q.h, 1)
                if ok(c - 1):
                    dve.wait_ge(q.hTh, j)
                    dve.tensor_tensor(hT_l[:, (c - 1) % 2, :], hT_p[(c - 1) % 2], hT_h[:, (c - 1) % 2, :].bitcast(f32),
                                      ALU.subtract).then_inc(q.hTl, 1)
                if ok(c - 2):
                    dve.wait_ge(q.yB, j - 1)
                    wait(dve, q.stored[c % 2], half_no(it, c - 2) * 16)
                    dve.tensor_tensor(y_out[:, c % 2, :], y_p[:, 0:D], yB[:, :], ALU.add).then_inc(q.y, 1)
            slot_turns(dve, turn)

        def attention_dve(dve):
            def norm(it, c):
                n = tile_no(it, c)
                combine(dve, 0, n, half_no(it, c) + 1, c % 2)
                wait_apart(dve, ffn[0].combined, n + 1, const_ready)
                dve.bn_stats(st6[:, 0, :], x_sb[:, ds(n, 1), :].rearrange("p a d -> p (a d)")).then_inc(a_bn, 1)
                wait_apart(dve, a_bn, n + 1, const_ready)
                dve.bn_aggr(mv[:, 0, :], st6[:, 0, :]).then_inc(a_stats, 1)

            def xn(it, c):
                n = tile_no(it, c)
                dve.wait_ge(a_rstd, n + 1)
                dve.tensor_scalar(out=xn_t[:, c % 2, :], in0=x_sb[:, ds(n, 1), :].rearrange("p a d -> p (a d)"),
                                  scalar1=mv[:, 0, 0:1], scalar2=rs[:, 0, 3:4], op0=ALU.subtract, op1=ALU.mult)\
                    .then_inc(a_xn, 1)

            def xa_lo(it, c):
                n = tile_no(it, c)
                dve.wait_ge(a_xah, n + 1)
                dve.tensor_tensor(xa[:, 1, :], xa_f[:, :], xa[:, 0, :].bitcast(f32), ALU.subtract).then_inc(a_xal, 1)

            def qk_lo(it, c):
                n = tile_no(it, c)
                dve.wait_ge(a_qkh, n + 1)
                for k in range(2):
                    ins = dve.scalar_tensor_tensor(out=qk_hl[:, k, 1, :], in0=MISC[:, P * (k + 1):P * (k + 2)],
                                                   scalar=bqk_sb[:, k:k + 1], in1=qk_hl[:, k, 0, :].bitcast(f32),
                                                   op0=ALU.add, op1=ALU.subtract)
                ins.then_inc(a_qkl, 1)

            def v_add(it, c):
                n = tile_no(it, c)
                dve.wait_ge(a_vp, n + 1)
                if it is None and n == 0:
                    dve.wait_ge(v_ones, 1)
                wait(dve, a_pv, n * 2 - 6 if not isinstance(n, int) or n >= 4 else 0)
                dve.tensor_tensor(v_st[:, c % 4, :, :, 0:HD],
                                  MISC[:, 3 * P:4 * P].rearrange("p (b c d) -> p b c d", b=NB, c=NC),
                                  bv_sb[:, :].rearrange("p (c d) -> p c d", c=NC).unsqueeze(1).to_broadcast([P, NB, NC, HD]),
                                  ALU.add).then_inc(a_v, 1)

            def row_max(it, c, u):
                n = tile_no(it, c)
                dve.wait_ge(a_s, n * 16 + u + 1)
                dve.tensor_reduce(mx[:, c % 2, u:u + 1], SB[u % 2][:, :], X, ALU.max).then_inc(a_max, 1)

            def reciprocals(it, c):
                n = tile_no(it, c)
                dve.wait_ge(a_nd, n * 32 + 32)
                dve.reciprocal(nd[:, 1, :], nd[:, 1, :]).then_inc(a_rec, 1)

            def vals_lo(it, c):
                n = tile_no(it, c)
                dve.wait_ge(a_vh, n + 1)
                dve.tensor_tensor(vh[:, 1, :], vals[:, :], vh[:, 0, :].bitcast(f32), ALU.subtract).then_inc(a_vl, 1)

            def project(it, c):
                n = tile_no(it, c)
                dve.wait_ge(a_oB, n + 1)
                wait(dve, a_x, n)
                dve.tensor_tensor(oA[:, :], MISC[:, P:2 * P], oB[:, :], ALU.add).then_inc(a_oA, 1)

            def turn(it, c):
                ok = lambda n: it is not None or 0 <= n < TILES
                for u in range(16):
                    if ok(c + 2):
                        row_max(it, c + 2, u)
                    if u == 0 and ok(c + 3):
                        qk_lo(it, c + 3)
                    if u == 2 and ok(c - 2):
                        reciprocals(it, c - 2)
                    if u == 4 and ok(c + 4):
                        norm(it, c + 4)
                    if u == 6 and ok(c + 3):
                        v_add(it, c + 3)
                    if u == 7 and ok(c - 2):
                        vals_lo(it, c - 2)
                    if u == 10 and ok(c - 2):
                        project(it, c - 2)
                    if u == 10 and ok(c + 4):
                        xn(it, c + 4)
                    if u == 14 and ok(c + 4):
                        xa_lo(it, c + 4)
            for_turns(dve, turn)

        def tensor_program(pe):
            pe.wait_ge(const_ready, 1)
            for f in range(2):
                route_pe(pe, f)
                slots_pe(pe, f)
                if f == 0:
                    attention_pe(pe)

        def route_pe(pe, f):
            q = ffn[f]
            for i in range(TILES // 4):
                pe.wait_ge(q.xn, i + 1)
                wait(pe, q.xlo, i)
                for k in range(4):
                    ins = pe.transpose(S0[:, P * k:P * (k + 1)], xn_all[:, 4 * i + k, :], ident[:, :])
                ins.then_inc(q.xT, 1)
                pe.wait_ge(q.xlo, i + 1)
                if i == 0 and f == 0:
                    pe.wait_ge(small_done, 1)
                wait(pe, q.lg, i)
                for k in range(4):
                    pe.matmul(S1[:, 16 * k:16 * k + 16], xr_h[:, P * k:P * (k + 1)], w_r[:, :], start=True, stop=False)
                    ins = pe.matmul(S1[:, 16 * k:16 * k + 16], xr_l[:, P * k:P * (k + 1)], w_r[:, :], start=False, stop=True)
                ins.then_inc(q.logit, 1)
            pe.wait_ge(q.sel, 1)
            flat = sel[:, :, :].rearrange("p n e -> p (n e)")
            pe.matmul(MISC[:, 0:P], upper[:, :], flat, start=True, stop=False)
            for s in range(1, TILES):
                pe.matmul(MISC[:, E * s:P], ones_b[:, :], flat[:, 0:P - E * s], start=False, stop=(s == TILES - 1))
            for n in range(TILES):
                ins = pe.matmul(MISC[:, P:P + E], ones_b[:, :], flat[:, E * n:E * n + E], start=(n == 0), stop=(n == TILES - 1))
            ins.then_inc(q.rank, 1)

        def slots_pe(pe, f):
            q = ffn[f]
            pe.wait_ge(q.slotw, 1)
            pe.wait_ge(w_lo_done, E)
            flat = w_exp[:, :, :].rearrange("p e c -> p (e c)")

            def turn(it, c):
                ok = lambda n: it is not None or 0 <= n < SLOTS
                j = tile_no(it, c)
                if ok(c):
                    w_up = pe.value_load(slot_w[0:1, ds(j, 1)], min_val=0, max_val=WE * (E - 1))
                if ok(c - 2):
                    w_down = pe.value_load(slot_w[0:1, ds(j - 2, 1)], min_val=0, max_val=WE * (E - 1))
                if ok(c):
                    wait(pe, q.xgl, j + 1)
                if ok(c + 1):
                    pe.wait_ge(q.xg[(c + 1) % 4], quarter_no(it, c + 1) * 16 + 16)
                    pe.transpose(xg_p, xg[:, (c + 1) % 4, :], ident[:, :]).then_inc(q.xgT, 1)
                if ok(c):
                    xh, xl = xg_h[:, c % 2, :], xg_l[:, c % 2, :]
                    for dst, free, done, base in ((gate_p[c % 2], q.silu, q.gate, 0), (up_p[c % 2], q.h, q.up, 1024)):
                        wait(pe, free, j - 1)
                        pe.matmul(dst, xh, flat[:, ds(w_up + base, F)], start=True, stop=False)
                        pe.matmul(dst, xh, flat[:, ds(w_up + (base + F), F)], start=False, stop=False)
                        pe.matmul(dst, xl, flat[:, ds(w_up + base, F)], start=False, stop=True).then_inc(done, 1)
                if ok(c - 1):
                    pe.wait_ge(q.h, j)
                    wait(pe, q.hTl, j - 2)
                    r = (c - 1) % 2
                    for k in range(4):
                        ins = pe.transpose(hT_p[r][:, P * k:P * (k + 1)], h_act[:, r, P * k:P * (k + 1)], ident[:, :])
                    ins.then_inc(q.hT, 1)
                if ok(c - 2):
                    pe.wait_ge(q.hTl, j - 1)
                    wait(pe, q.y, j - 2)
                    r = c % 2
                    for k in range(4):
                        for part, src in enumerate((hT_h, hT_l)):
                            ins = pe.matmul(y_p, src[:, r, P * k:P * (k + 1)], flat[:, ds(w_down + (2048 + 256 * k), 2 * D)],
                                            start=(k == 0 and part == 0), stop=(k == 3 and part == 1))
                    ins.then_inc(q.outp, 1)
            slot_turns(pe, turn)

        def attention_pe(pe):
            def cols(t, b, c=None):
                t = t[:, b, :]
                return t if c is None else t[:, P * c:P * (c + 1)]

            def scores_for_max(it, c, u):
                n, r = tile_no(it, c), c % 4
                b, ch = u // NC, u % NC
                if ch == 0:
                    if b == 0:
                        pe.wait_ge(a_stacked[r], quarter_no(it, c) * 16 + 16)
                    pe.wait_ge(a_qz[b], n * 16 + 16)
                wait(pe, a_max, n * 16 + u - 1)
                pe.matmul(SB[u % 2][:, :], qz[:, b, P * ch:P * (ch + 1)], k_st(r), start=True, stop=True).then_inc(a_s, 1)

            def scores(it, c, k):
                n, r = tile_no(it, c), c % 4
                cp, b = k // NB, k % NB
                if k == 0:
                    pe.wait_ge(a_mrow[r], quarter_no(it, c) * 64 + 64)
                if cp == 0:
                    pe.wait_ge(a_kz, n * NB + b + 1)
                wait(pe, a_exp, n * 8 + k - 1)
                for cc in range(2):
                    ch = 2 * cp + cc
                    ins = pe.matmul(ST[k % 2][:, 512 * cc:512 * (cc + 1)], kz[:, b, P * ch:P * (ch + 1)], q_st(r),
                                    start=True, stop=True)
                ins.then_inc(a_st, 1)

            def values(it, c, cp, cc):
                n = tile_no(it, c)
                if cc == 0:
                    pe.wait_ge(a_exp, n * 8 + 4 * cp + 4)
                if cp == 0 and cc == 0:
                    pe.wait_ge(a_v, n + 1)
                    wait(pe, a_o, n)
                for b in range(NB):
                    ins = pe.matmul(PVB[32 * b:32 * b + 32, :], v_st[:, c % 4, b, 2 * cp + cc, :], prob[:, cp, b, cc, :],
                                    start=(cp == 0 and cc == 0), stop=(cp == 1 and cc == 1))
                if cc == 1:
                    ins.then_inc(a_pv, 1)

            def max_t(it, c):
                n = tile_no(it, c)
                pe.wait_ge(a_max, n * 16 + 16)
                if it is not None or n + 2 < TILES:
                    pe.wait_ge(a_qkl, n + 3)
                else:
                    pe.wait_ge(a_oA, n - 3)
                pe.transpose(MISC[0:NB * NC, 0:P], mx[:, c % 2, :], ident[:, :]).then_inc(a_mT, 1)

            def x_t(it, c):
                n = tile_no(it, c)
                pe.wait_ge(a_xn, n + 1)
                if it is not None or n >= 6:
                    pe.wait_ge(a_oA, n - 5)
                else:
                    wait(pe, a_v, n)
                pe.transpose(MISC[:, 0:P], xn_t[:, c % 2, :], ident[:, :]).then_inc(a_xT, 1)

            def qk(it, c):
                n = tile_no(it, c)
                pe.wait_ge(a_xal, n + 1)
                for k in range(2):
                    o = MISC[:, P * (k + 1):P * (k + 2)]
                    pe.matmul(o, w_qk[:, k, 0, :], xa[:, 0, :], start=True, stop=False)
                    pe.matmul(o, w_qk[:, k, 0, :], xa[:, 1, :], start=False, stop=False)
                    ins = pe.matmul(o, w_qk[:, k, 1, :], xa[:, 0, :], start=False, stop=True)
                ins.then_inc(a_qk, 1)

            def v(it, c):
                n = tile_no(it, c)
                if it is not None or n >= 2:
                    pe.wait_ge(a_negm, n - 1)
                else:
                    pe.wait_ge(a_qkl, n + 1)
                wv = w_small[:, 3 * D:4 * D].rearrange("p (i c) -> p i c", i=GC)
                for b in range(NB):
                    for g in range(GC):
                        ins = pe.matmul(MISC[32 * g:32 * g + 32, 3 * P + 32 * b:3 * P + 32 * b + 32],
                                        xa_f[:, BLK * b:BLK * (b + 1)], wv[:, g, :], start=True, stop=True)
                ins.then_inc(a_vp, 1)

            def project(it, c):
                n = tile_no(it, c)
                pe.wait_ge(a_vl, n + 1)
                if it is not None or n + 5 < TILES:
                    pe.wait_ge(a_v, n + 6)
                elif n + 3 < TILES:
                    pe.wait_ge(a_negm, n + 4)
                pe.matmul(MISC[:, P:3 * P], vh[:, 0, :], w_o[:, :], start=True, stop=False)
                pe.matmul(MISC[:, P:3 * P], vh[:, 1, :], w_o[:, :], start=False, stop=True).then_inc(a_op, 1)

            def turn(it, c):
                ok = lambda n: it is not None or 0 <= n < TILES
                for k in range(8):
                    if k == 1 and ok(c + 1):
                        max_t(it, c + 1)
                    if ok(c):
                        scores(it, c, k)
                    if ok(c + 2):
                        scores_for_max(it, c + 2, 2 * k)
                        scores_for_max(it, c + 2, 2 * k + 1)
                    if k < 2 and ok(c - 1):
                        values(it, c - 1, 1, k)
                    if k == 2 and ok(c + 3):
                        v(it, c + 3)
                    if k == 4 and ok(c - 2):
                        project(it, c - 2)
                    if k == 6 and ok(c + 4):
                        x_t(it, c + 4)
                    if 5 <= k < 7 and ok(c):
                        values(it, c, 0, k - 5)
                    if k == 7 and ok(c + 4):
                        qk(it, c + 4)
            for_turns(pe, turn)

        block = ctx.enter_context(nc.Block())
        block.sync(sync_program)
        block.gpsimd(gpsimd_program)
        block.scalar(scalar_program)
        block.vector(vector_program)
        block.tensor(tensor_program)


_OUT_SHAPE = (B, S, D)


def kernel(**inputs):
    import numpy as np
    import concourse.bacc as bacc
    from concourse.bass_utils import run_bass_kernel_spmd as run

    nc = bacc.Bacc("TRN2", target_bir_lowering=False, num_devices=1)
    i = {k.replace("L0_", ""): np.asarray(v) for k, v in inputs.items()}
    w = i["attn_Wqkv"].reshape(G, 3, HD, D)
    b = i["attn_bqkv"].reshape(G, 3, HD)
    wq, wk = (w[:, k].transpose(2, 1, 0).reshape(D, D) for k in (0, 1))
    wo = i["attn_Wo"].reshape(D, G, HD).transpose(2, 1, 0).reshape(D, D)
    wv = w[:, 2].reshape(NC, GC, HD, D).transpose(3, 1, 0, 2).reshape(D, D)
    bv = b[:, 2].reshape(NC, GC, HD).transpose(1, 0, 2).reshape(GC, 1, NC * HD)
    arrays = {
        "x": i["attn_x"].reshape(B * S, D),
        "w_gate_up": np.stack([i["ffn_We_gate"], i["ffn_We_in"]], axis=1),
        "w_down": i["ffn_We_out"],
        "w_att": np.concatenate([wq, wk, wo, wv, i["ffn_W_gate"]], axis=1),
        "b_qk": b[:, 0:2].transpose(2, 0, 1).reshape(D, 2),
        "b_v": np.broadcast_to(bv, (GC, BLK, NC * HD)).reshape(P, NC * HD),
        "b_o": np.broadcast_to(i["attn_bo"][None, :], (P, D)),
    }
    arrays = {f"in_{k}": np.ascontiguousarray(v) for k, v in arrays.items()}
    f32 = mybir.dt.float32
    aps = {k: nc.dram_tensor(k, v.shape, f32, kind="ExternalInput").ap() for k, v in arrays.items()}
    out = nc.dram_tensor("out", (B * S, D), f32, kind="ExternalOutput").ap()
    scratch = [nc.dram_tensor(n, s, f32, kind="Internal").ap() for n, s in (
        ("slot_x", (SLOTS * P, D)), ("slot_y", (SLOTS * P, D)), ("qk_hop", (2, 2, P, S)),
        ("max_hop", (NB * NC, P)), ("att_hop", (P, S)))]
    macaron_kernel(nc, aps["in_x"], aps["in_w_gate_up"], aps["in_w_down"], aps["in_w_att"], None,
                   aps["in_b_qk"], aps["in_b_v"], aps["in_b_o"], out, *scratch)
    r = run(nc, [arrays], core_ids=[0])
    return r.results[0]["out"].reshape(_OUT_SHAPE)
```

```python
import concourse.bass as bass
from concourse import mybir
from contextlib import ExitStack

B, S, D = 4, 512, 128
HEADS, HD = 16, 8
F, E = 512, 8
P = 128
TILES = B * S // P
SLOTS = -(-(2 * TILES + E - 1) // 4) * 4
BLK = S // HEADS
NB = P // BLK
G = D // HD
GC = P // BLK
NC = G // GC
KROWS = 3 * HD
WE = 3072
EPS = 1e-5
COPIES = 2 * TILES
RING = 8
PADS = RING * P


def tile_no(it, c):
    return c if it is None else it * 4 + c


def half_no(it, c):
    return c // 2 if it is None else it * 2 + c // 2


def quarter_no(it, c):
    return c // 4 if it is None else it + c // 4


def slot_no(it, c):
    return c if it is None else it * RING + c


def slot_half_no(it, c):
    return c // 2 if it is None else it * (RING // 2) + c // 2


def slot_ring_no(it, c):
    return c // RING if it is None else it + c // RING


def wait(eng, sem, value):
    if isinstance(value, int) and value <= 0:
        return
    eng.wait_ge(sem, value)


def wait_apart(eng, sem, value, ready):
    value = value if isinstance(value, int) else eng.snap(value)
    eng.wait_ge(ready, 1)
    eng.wait_ge(sem, value)


def macaron_kernel(nc, x_in, w_gate_up, w_down, w_att, b_qk, b_v, b_o, out,
                   x_tok, y_tok, qk_hop, max_hop, att_hop):
    f32, f32r, bf16 = mybir.dt.float32, mybir.dt.float32r, mybir.dt.bfloat16
    i32, u32 = mybir.dt.int32, mybir.dt.uint32
    ALU = mybir.AluOpType
    ACT = mybir.ActivationFunctionType
    X = mybir.AxisListType.X
    ds = bass.ds

    ctx = ExitStack()
    with ctx:
        def sb(name, shape, dt=f32):
            return ctx.enter_context(nc.sbuf_tensor(name, shape, dt))

        def ps(name, shape):
            return ctx.enter_context(nc.psum_tensor(name, shape, f32))

        def sem(name):
            return ctx.enter_context(nc.semaphore(name))

        x_sb = sb("x_sb", [P, TILES, D])
        w_exp = sb("w_exp", [P, E, WE], f32r)
        big = sb("big", [P, 8192])
        stack = sb("stack", [P, 4096], f32r)
        xn_v = sb("xn_v", [P, TILES * D])
        qz = sb("qz", [P, NB, S], f32r)
        kz = sb("kz", [P, NB, S], f32r)
        xT_split = sb("xT_split", [P, 512], f32r)
        w_small = sb("w_small", [P, 4 * D + E])
        w_qk = sb("w_qk", [P, 2, 2, D], f32r)
        w_o = sb("w_o", [P, 2 * D], f32r)
        w_r = sb("w_r", [P, 2 * E], f32r)
        bqk_sb = sb("bqk_sb", [P, 2])
        bv_sb = sb("bv_sb", [P, NC * HD])
        bo_sb = sb("bo_sb", [P, D])
        ident = sb("ident", [P, P])
        upper = sb("upper", [P, P], bf16)
        ones_b = sb("ones_b", [P, P], bf16)
        rev = sb("rev", [P, E])
        thr = sb("thr", [P, TILES])
        slot_j = sb("slot_j", [1, SLOTS])
        before = sb("before", [P, E, E])
        halves = sb("halves", [P, 3, TILES])
        carrier = sb("carrier", [P, 2 * RING])
        st6 = sb("st6", [P, TILES + 1, 6])
        mv = sb("mv", [P, TILES + 1, 2])
        rs = sb("rs", [P, TILES + 1, 4])
        lgB = sb("lgB", [P, TILES, E])
        lg = sb("lg", [P, TILES, E])
        one1 = sb("one1", [P, TILES, E])
        one2 = sb("one2", [P, TILES, E])
        sel = sb("sel", [P, TILES, E], bf16)
        m1 = sb("m1", [P, TILES])
        m2 = sb("m2", [P, TILES])
        kk = sb("kk", [P, TILES])
        e2 = sb("e2", [P, TILES])
        n_e = sb("n_e", [P, E])
        sl_e = sb("sl_e", [P, E])
        off = sb("off", [P, E])
        offs = sb("offs", [P, E])
        incl = sb("incl", [P, E])
        mm = sb("mm", [P, E, E])
        se = sb("se", [1, SLOTS, E])
        sef = sb("sef", [1, SLOTS])
        slot_w = sb("slot_w", [1, SLOTS], i32)
        posf = sb("posf", [P, TILES, 2])
        wts = sb("wts", [P, TILES, 2])
        row_now = sb("row_now", [P, RING], u32)
        thr_j = sb("thr_j", [P, SLOTS + 1])
        col = sb("col", [P, P])
        no_a = sb("no_a", [P, TILES, 2])
        no_p = sb("no_p", [P, 1])
        pad_no = sb("pad_no", [P, SLOTS])
        slot_at = sb("slot_at", [P, COPIES])
        row_at = sb("row_at", [P, COPIES])
        idx_f = sb("idx_f", [P, 2, SLOTS])
        idx = sb("idx", [P, SLOTS + 1], u32)
        yg = sb("yg", [P, 2, 2, D])
        xn_t = sb("xn_t", [P, 2, D])
        xa_f = sb("xa_f", [P, P])
        xa = sb("xa", [P, 2, P], f32r)
        qk_hl = sb("qk_hl", [P, 2, 2, P], f32r)
        mx = sb("mx", [P, 2, NB * NC])
        neg_m = sb("neg_m", [NB * NC, P], f32r)
        o_sb = sb("o_sb", [P, S])
        nd = sb("nd", [P, 2, P])
        vals = sb("vals", [P, P])
        vh = sb("vh", [P, 2, P], f32r)
        oB = sb("oB", [P, P])
        oA = sb("oA", [P, P])

        r1, r2 = (o_sb[:, P * k:P * (k + 1)].rearrange("p (n e) -> p n e", e=E) for k in range(2))
        cmp = o_sb[:, 2 * P:3 * P].rearrange("p (e n) -> p e n", e=E)
        yB = oB
        xn_all = xn_v[:, :].rearrange("p (n d) -> p n d", n=TILES)
        v_st = xn_v[:, :].rearrange("p (r b c d) -> p r b c d", r=4, b=NB, c=NC)
        stage = big[:, 0:4 * 1536].rearrange("p (r c) -> p r c", r=4)
        ge = big[:, 6144:6144 + COPIES * (SLOTS + 1) // 2].bitcast(bf16).rearrange("p (m j) -> p m j", m=COPIES)
        hot_j = big[:, 6912:6912 + COPIES * SLOTS].bitcast(bf16).rearrange("p (m h j) -> p m h j", m=COPIES, h=2)
        hot_r = xn_v[:, :].bitcast(bf16).rearrange("p (m r) -> p m r", m=COPIES)
        xg = big[:, 0:RING * D].rearrange("p (r c) -> p r c", r=RING)
        s_act = big[:, 1024:2048].rearrange("p (r c) -> p r c", r=2)
        h_act = big[:, 2048:3072].rearrange("p (r c) -> p r c", r=2)
        y_out = big[:, 3072:3328].rearrange("p (r c) -> p r c", r=2)
        y_all = big[:, 4096:8192].rearrange("p (n k d) -> p n k d", n=TILES, k=2)
        prob = big[:, :].rearrange("p (a b c s) -> p a b c s", a=2, b=NB, c=2)
        hT_h = stack[:, 0:1024].rearrange("p (r c) -> p r c", r=2)
        hT_l = stack[:, 1024:2048].rearrange("p (r c) -> p r c", r=2)
        xg_h = xT_split[:, 0:256].rearrange("p (r c) -> p r c", r=2)
        xg_l = xT_split[:, 256:512].rearrange("p (r c) -> p r c", r=2)
        xr_h, xr_l = ([stack[:, 1024 * (r + 1) + 512 * part:1024 * (r + 1) + 512 * (part + 1)] for r in range(2)]
                      for part in range(2))
        def q_st(r):
            return stack[:, 1024 * r:1024 * r + S]

        def k_st(r):
            return stack[:, 1024 * r + S:1024 * r + 2 * S]

        S0 = ps("S0", [P, 512])
        S1 = ps("S1", [P, 512])
        ST0 = ps("ST0", [P, 1024])
        ST1 = ps("ST1", [P, 1024])
        PVB = ps("PVB", [P, 512])
        MISC = ps("MISC", [P, 512])
        SB = [S0, S1]
        ST = [ST0, ST1]
        gate_p = [S0[:, :], S1[:, :]]
        up_p = [ST0[:, 0:512], ST0[:, 512:1024]]
        hT_p = [ST1[:, 0:512], ST1[:, 512:1024]]
        xg_p = PVB[:, 0:P]
        y_p = MISC[:, 0:2 * D]
        logit_p = MISC[:, 256:512].rearrange("p (k h e) -> p k h e", k=TILES, h=2)

        x_loaded, small_loaded, w_raw = sem("x_loaded"), sem("small_loaded"), [sem(f"w_raw{i}") for i in range(4)]
        init_ready, zeroed, hop_init = sem("init_ready"), sem("zeroed"), sem("hop_init")
        a_qz, a_kz, v_ones = [sem(f"a_qz{b}") for b in range(NB)], sem("a_kz"), sem("v_ones")
        const_ready, pool_step = sem("const_ready"), sem("pool_step")
        w_hi_done, w_lo_dve, w_lo_pool = sem("w_hi_done"), sem("w_lo_dve"), sem("w_lo_pool")
        LO_DVE, LO_POOL = (0, 1, 7), (2, 3, 4, 5, 6)
        small_hi, small_done = sem("small_hi"), sem("small_done")
        dve_step = sem("dve_step")

        xg_sems = [sem(f"xg{r}") for r in range(RING)]

        class Phase:
            def __init__(self, f):
                self.stats, self.rstd, self.xn, self.xT = (
                    sem(f"stats_{f}"), sem(f"rstd_{f}"), sem(f"xn_{f}"), sem(f"xT_{f}"))
                self.xhi, self.xlo, self.logit, self.lgB = (
                    sem(f"xhi_{f}"), sem(f"xlo_{f}"), sem(f"logit_{f}"), sem(f"lgB_{f}"))
                self.lg, self.gap, self.exp2, self.sel = (
                    sem(f"lg_{f}"), sem(f"gap_{f}"), sem(f"exp2_{f}"), sem(f"sel_{f}"))
                self.rank, self.slotw = sem(f"rank_{f}"), sem(f"slotw_{f}")
                self.xgT, self.xgh, self.xgl, self.gate = (
                    sem(f"xgT_{f}"), sem(f"xgh_{f}"), sem(f"xgl_{f}"), sem(f"gate_{f}"))
                self.up, self.silu, self.h, self.hT = (
                    sem(f"up_{f}"), sem(f"silu_{f}"), sem(f"h_{f}"), sem(f"hT_{f}"))
                self.hTh, self.hTl, self.outp, self.yB = (
                    sem(f"hTh_{f}"), sem(f"hTl_{f}"), sem(f"outp_{f}"), sem(f"yB_{f}"))
                self.y, self.half, self.combined = (
                    sem(f"y_{f}"), sem(f"half_{f}"), sem(f"combined_{f}"))
                self.xg = xg_sems
                self.xg_base = 16 * (SLOTS // RING) * f
                self.stored = [sem(f"stored{r}_{f}") for r in range(2)]
                self.gathered = [sem(f"gathered{r}_{f}") for r in range(2 + 2 * f)]
                self.row_now, self.rows, self.hot, self.inv, self.idx = (
                    sem(f"row_now_{f}"), sem(f"rows_{f}"), sem(f"hot_{f}"), sem(f"inv_{f}"), sem(f"idx_{f}"))

        ffn = [Phase(0), Phase(1)]
        a_stats, a_rstd, a_xn, a_xT, a_xah, a_xal = map(sem, (
            "a_stats", "a_rstd", "a_xn", "a_xT", "a_xah", "a_xal"))
        a_qk, a_qkh, a_qkl, a_vp, a_v = map(sem, ("a_qk", "a_qkh", "a_qkl", "a_vp", "a_v"))
        a_hop = sem("a_hop")
        a_stacked = [sem(f"a_stacked{r}") for r in range(4)]
        a_s, a_max = sem("a_s"), sem("a_max")
        a_mT, a_negm, a_mhop = sem("a_mT"), sem("a_negm"), sem("a_mhop")
        a_mrow = [sem(f"a_mrow{r}") for r in range(4)]
        a_st, a_exp, a_pv, a_o = sem("a_st"), sem("a_exp"), sem("a_pv"), sem("a_o")
        a_ohop, a_nd = sem("a_ohop"), sem("a_nd")
        a_vals, a_vh, a_vl, a_op, a_oB, a_oA, a_x = map(sem, (
            "a_vals", "a_vh", "a_vl", "a_op", "a_oB", "a_oA", "a_x"))
        stored_out = sem("stored_out")
        a_pool_step, a_ob, a_bn, a_rec = map(sem, ("a_pool_step", "a_ob", "a_bn", "a_rec"))

        def wait_low_part(eng, e):
            if e in LO_DVE:
                eng.wait_ge(w_lo_dve, LO_DVE.index(e) + 1)
            else:
                eng.wait_ge(w_lo_pool, LO_POOL.index(e) + 1)

        def low_part(eng, e):
            eng.wait_ge(w_hi_done, e + 1)
            we, r = w_exp[:, e, :], e % 4
            gu = we[:, 0:2048].rearrange("p (k h f) -> p k h f", k=2, h=2)
            dn = we[:, 2048:3072].rearrange("p (c h d) -> p c h d", c=4, h=2)
            eng.tensor_tensor(out=gu[:, :, 1, :], in0=stage[:, r, 0:1024].rearrange("p (k f) -> p k f", k=2),
                              in1=gu[:, :, 0, :].bitcast(f32), op=ALU.subtract)
            return eng.tensor_tensor(out=dn[:, :, 1, :], in0=stage[:, r, 1024:1536].rearrange("p (c d) -> p c d", c=4),
                                     in1=dn[:, :, 0, :].bitcast(f32), op=ALU.subtract)

        class Steps:
            def __init__(self, eng, s):
                self.eng, self.s, self.n = eng, s, 0

            def link(self, ins):
                self.n += 1
                ins.then_inc(self.s, 1)
                self.eng.wait_ge(self.s, self.n)

        def sync_program(sp):
            sp.dma_start(x_sb[:, :, :], x_in.rearrange("(n p) d -> p n d", p=P)).then_inc(x_loaded, 16)
            sp.dma_start(w_small[:, :], w_att).then_inc(small_loaded, 16)
            sp.dma_start(bqk_sb[:, :], b_qk).then_inc(small_loaded, 16)
            sp.dma_start(bv_sb[:, :], b_v).then_inc(small_loaded, 16)
            sp.dma_start(bo_sb[:, :], b_o).then_inc(small_loaded, 16)

            def expert_weights(e):
                r = e % 4
                if e >= 4:
                    wait_low_part(sp, e - 4)
                sp.dma_start(stage[:, r, 0:1024].rearrange("p (k f) -> p k f", k=2),
                             w_gate_up[e:e + 1].rearrange("e k p f -> p (e k) f")).then_inc(w_raw[r], 16)
                sp.dma_start(stage[:, r, 1024:1536].rearrange("p (c d) -> p c d", c=4),
                             w_down[e:e + 1].rearrange("e (c p) d -> p (e c) d", p=P)).then_inc(w_raw[r], 16)

            for e in range(4):
                expert_weights(e)
            sp.wait_ge(init_ready, 1)
            for r in range(2):
                sp.dma_start(qk_hop[r].rearrange("k p s -> p k s"),
                             stack[:, 0:2 * S].rearrange("p (k s) -> p k s", k=2).bitcast(f32)).then_inc(hop_init, 16)
            sp.wait_ge(init_ready, 2)
            sp.dma_start(x_tok[0:PADS, :].rearrange("(n p) d -> p n d", p=P),
                         kz[:, 0:2, :].rearrange("p a (b d) -> p (a b) d", d=D).bitcast(f32)).then_inc(zeroed, 16)
            publish(sp, 0)
            for e in range(4, E):
                expert_weights(e)
            sp.wait_ge(hop_init, 32)
            for r in range(2):
                sp.wait_ge(ffn[0].stored[r], 16 * SLOTS // 2)
            attention_sp(sp)
            publish(sp, 1)
            q = ffn[1]
            for r in range(2):
                sp.wait_ge(q.stored[r], 16 * SLOTS // 2)
            for i in range(4):
                for k in range(2):
                    sp.dma_start(y_all[:, 4 * i:4 * i + 4, k, :],
                                 y_tok[PADS + k * B * S + 4 * i * P:PADS + k * B * S + 4 * (i + 1) * P, :].rearrange("(n p) d -> p n d", p=P))\
                        .then_inc(q.gathered[i], 16)
            for i in range(4):
                sp.wait_ge(q.combined, 4 * i + 4)
                sp.dma_start(out.rearrange("(n p) d -> p n d", p=P)[:, 4 * i:4 * i + 4, :],
                             x_sb[:, 4 * i:4 * i + 4, :]).then_inc(stored_out, 16)
            sp.wait_ge(stored_out, 16 * 4)

        def publish(sp, f):
            q = ffn[f]
            sp.wait_ge(q.xn, GROUPS)
            for k in range(2):
                sp.dma_start(x_tok[PADS + k * B * S:PADS + (k + 1) * B * S, :].rearrange("(n p) d -> p n d", p=P), xn_all)\
                    .then_inc(q.rows, 16)

        def attention_sp(sp):
            def results(it, c):
                n, r = tile_no(it, c), c % 2
                wait(sp, ffn[0].combined, n - 1)
                sp.dma_start(yg[:, r, :, :], y_tok[PADS:, :].rearrange("(k n p) d -> n p k d", k=2, p=P)[ds(n, 1)]
                             .rearrange("n p k d -> p (n k) d")).then_inc(ffn[0].gathered[r], 16)

            def qk_write(it, c):
                n = tile_no(it, c)
                sp.wait_ge(a_qkl, n + 1)
                rows = qk_hop[c % 2].rearrange("k (b r) (g t) -> k (r g) b t", b=NB, g=G)
                for k, part, h in ((0, 0, 0), (0, 1, 1), (0, 2, 0), (1, 0, 0), (1, 1, 0), (1, 2, 1)):
                    sp.dma_start(rows[k, P * part:P * (part + 1)],
                                 qk_hl[:, k, h, :].rearrange("p (b t) -> p b t", t=BLK).bitcast(f32)).then_inc(a_hop, 16)

            def qk_read(it, c):
                n, r = tile_no(it, c), c % 4
                sp.wait_ge(a_hop, n * 96 + 96)
                wait(sp, a_st, n * 8 - 24 if not isinstance(n, int) or n >= 4 else 0)
                sp.dma_start(stack[:, 1024 * r:1024 * (r + 1)].rearrange("p (k s) -> p k s", k=2).bitcast(f32),
                             qk_hop[c % 2].rearrange("k p s -> p k s")).then_inc(a_stacked[r], 16)

            def fill_qz(it, c, b):
                n = tile_no(it, c)
                wait(sp, a_s, n * 16 + NC * b - 12)
                sp.dma_start(qz[32 * b:32 * b + KROWS, b, :].bitcast(f32), qk_hop[c % 2, 0, 32 * b:32 * b + KROWS, :])\
                    .then_inc(a_qz[b], 16)

            def max_write(it, c):
                if it is not None or c > 0:
                    sp.wait_ge(a_mrow[(c - 1) % 4], quarter_no(it, c - 1) * 64 + 64)
                sp.wait_ge(a_negm, tile_no(it, c) + 1)
                sp.dma_start(max_hop, neg_m[:, :].bitcast(f32)).then_inc(a_mhop, 16)

            def max_read(it, c):
                n, r = tile_no(it, c), c % 4
                sp.wait_ge(a_mhop, n * 16 + 16)
                for b in range(NB):
                    row = 32 * b + KROWS
                    sp.dma_start(q_st(r)[row:row + 1, :].bitcast(f32),
                                 max_hop[NC * b:NC * (b + 1), :].rearrange("(o a) s -> o (a s)", o=1))\
                        .then_inc(a_mrow[r], 16)

            def out_write(it, c):
                sp.wait_ge(a_o, tile_no(it, c) + 1)
                sp.dma_start(att_hop, o_sb[:, :]).then_inc(a_ohop, 16)

            def out_read(it, c):
                n = tile_no(it, c)
                sp.wait_ge(a_ohop, n * 16 + 16)
                wait(sp, a_vals, n)
                src = att_hop.rearrange("(b k d) (g t) -> k (d g) b t", b=NB, k=4, g=G)
                for k in range(2):
                    sp.dma_start(nd[:, k, :].rearrange("p (b t) -> p b t", b=NB), src[k]).then_inc(a_nd, 16)

            def turn(it, c):
                ok = lambda n: it is not None or 0 <= n < TILES
                if ok(c + 2):
                    fill_qz(it, c + 2, 3)
                if ok(c + 5):
                    results(it, c + 5)
                if ok(c + 3):
                    qk_write(it, c + 3)
                if ok(c + 1):
                    max_write(it, c + 1)
                if ok(c + 1):
                    max_read(it, c + 1)
                if ok(c + 3):
                    qk_read(it, c + 3)
                if ok(c - 1):
                    out_write(it, c - 1)
                if ok(c + 3):
                    fill_qz(it, c + 3, 0)
                    fill_qz(it, c + 3, 1)
                if ok(c - 1):
                    out_read(it, c - 1)
                if ok(c + 3):
                    fill_qz(it, c + 3, 2)

            results(None, 0)
            for_turns(sp, turn)

        def for_turns(eng, turn):
            for c in range(-4, 3):
                turn(None, c)
            with eng.Fori(0, TILES // 4 - 2) as it:
                for c in range(3, 7):
                    turn(it, c)
            for c in range(TILES - 5, TILES + 2):
                turn(None, c)

        def gpsimd_program(pool):
            st = Steps(pool, pool_step)
            st.link(pool.memset(ident[:, :], 0.0))
            pool.memset(ones_b[:, :], 1.0)
            st.link(pool.memset(before[:, :, :], 1.0))
            for k, value in enumerate((-0.5, 1.5, EPS)):
                ins = pool.memset(halves[:, k, :], value)
            st.link(ins)
            pool.affine_select(out=ident[:, :], in_=ident[:, :], compare_op=ALU.not_equal, fill=1.0,
                               base=0, pattern=[[-1, P]], channel_multiplier=1)
            pool.affine_select(out=upper[:, :], in_=ones_b[:, :], compare_op=ALU.is_gt, fill=0.0,
                               base=0, pattern=[[1, P]], channel_multiplier=-1)
            pool.affine_select(out=before[:, :, :], in_=before[:, :, :], compare_op=ALU.is_gt, fill=0.0,
                               base=0, pattern=[[1, E], [-1, E]], channel_multiplier=0)
            pool.iota(rev[:, :], pattern=[[-1, E]], base=E, channel_multiplier=0,
                      allow_small_or_imprecise_dtypes=True)
            pool.iota(thr[:, :], pattern=[[P, TILES]], base=0, channel_multiplier=0,
                      allow_small_or_imprecise_dtypes=True)
            for table, pattern, base, by_row in (
                    (thr_j[:, :], [[P, SLOTS + 1]], 0, 0), (col[:, :], [[1, P]], -P, 0),
                    (no_a[:, :, :], [[1, TILES], [TILES, 2]], 1, 0), (no_p[:, :], [[1, 1]], 0, 1),
                    (pad_no[:, :], [[0, SLOTS // RING], [P, RING]], P - PADS, 1)):
                pool.iota(table, pattern=pattern, base=base, channel_multiplier=by_row,
                          allow_small_or_imprecise_dtypes=True)
            pool.iota(slot_j[:, :], pattern=[[1, SLOTS]], base=0, channel_multiplier=0,
                      allow_small_or_imprecise_dtypes=True).then_inc(const_ready, 1)
            pool.wait_ge(const_ready, 1)

            for f in range(2):
                if f == 0:
                    rstd_pool(pool, st, f, 0)
                rstd_pool(pool, st, f, 1)
                if f == 0:
                    pool.memset(stack[:, 0:S].bitcast(f32), 0.0)
                    pool.memset(stack[:, S:2 * S].bitcast(f32), 1.0).then_inc(init_ready, 1)
                    pool.memset(qz[:, :, :].bitcast(f32), 0.0)
                    pool.memset(kz[:, :, :].bitcast(f32), 0.0).then_inc(init_ready, 1)
                    for e in LO_POOL:
                        low_part(pool, e).then_inc(w_lo_pool, 1)
                slots_pool(pool, f)
                if f == 0:
                    attention_pool(pool, st)

        def rstd_chain(pool, link, m, r):
            c = [halves[:, k, 0:m.shape[1]] for k in range(3)]
            link(pool.tensor_tensor(out=r[:, :, 1], in0=m[:, :, 1], in1=c[2], op=ALU.add))
            link(pool.tensor_tensor(out=r[:, :, 0], in0=r[:, :, 1], in1=c[0], op=ALU.pow))
            link(pool.tensor_tensor(out=r[:, :, 2], in0=r[:, :, 0], in1=r[:, :, 0], op=ALU.mult))
            link(pool.tensor_tensor(out=r[:, :, 2], in0=r[:, :, 2], in1=r[:, :, 1], op=ALU.mult))
            link(pool.tensor_tensor(out=r[:, :, 2], in0=r[:, :, 2], in1=c[0], op=ALU.mult))
            link(pool.tensor_tensor(out=r[:, :, 2], in0=r[:, :, 2], in1=c[1], op=ALU.add))
            return pool.tensor_tensor(out=r[:, :, 3], in0=r[:, :, 2], in1=r[:, :, 0], op=ALU.mult)

        GROUPS = TILES // 4
        BATCHES = ((0, GROUPS - 1), (GROUPS - 1, GROUPS))

        def rstd_pool(pool, st, f, batch):
            q = ffn[f]
            first, last = BATCHES[batch]
            pool.wait_ge(q.stats, last)
            rstd_chain(pool, st.link, mv[:, 4 * first:4 * last, :], rs[:, 4 * first:4 * last, :]).then_inc(q.rstd, 1)

        def slots_pool(pool, f):
            q = ffn[f]

            def copy_index(it, c):
                j, r = slot_no(it, c), c % RING
                pool.tensor_copy(out=row_now[:, r:r + 1], in_=idx[:, ds(j, 1)]).then_inc(q.row_now, 1)

            def fetch(it, c):
                j, r = slot_no(it, c), c % RING
                wait(pool, q.stored[(c + 1) % 2], (slot_half_no(it, c + 1) - 3) * 16)
                wait(pool, q.xgT, j - RING + 1)
                pool.wait_ge(q.row_now, j + 1)
                pool.tensor_tensor(out=carrier[:, r:r + 1], in0=halves[:, 0, 0:1], in1=halves[:, 0, 0:1], op=ALU.add)
                copy_index(it, c + 1)
                pool.indirect_dma_start(xg[:, r, :], None, x_tok,
                                        bass.IndirectOffsetOnAxis(ap=row_now[:, r:r + 1], axis=0)).then_inc(q.xg[r], 16)

            def send(it, c):
                j, r = slot_no(it, c), c % RING
                pool.wait_ge(q.y, j + 1)
                pool.tensor_tensor(out=carrier[:, RING + r:RING + r + 1], in0=halves[:, 0, 0:1], in1=halves[:, 0, 0:1],
                                   op=ALU.add)
                pool.indirect_dma_start(y_tok, bass.IndirectOffsetOnAxis(ap=row_now[:, r:r + 1], axis=0),
                                        y_out[:, c % 2, :], None).then_inc(q.stored[c % 2], 16)

            pool.wait_ge(q.idx, 1)
            pool.wait_ge(q.rows, 32)
            pool.wait_ge(zeroed, 16)
            if f == 0:
                pool.wait_ge(w_lo_dve, len(LO_DVE))
            else:
                pool.wait_ge(a_pv, 2 * TILES)
            ahead = RING - 3
            copy_index(None, 0)
            for c in range(ahead):
                fetch(None, c)
            for c in range(3):
                fetch(None, c + ahead)
                send(None, c)
            with pool.Fori(0, SLOTS // RING - 1) as it:
                for c in range(3, RING + 3):
                    fetch(it, c + ahead)
                    send(it, c)
            for c in range(SLOTS - ahead, SLOTS):
                send(None, c)

        def attention_pool(pool, st):
            pool.wait_ge(ffn[0].inv, 1)
            pool.memset(v_st[:, :, :, :, :], 1.0).then_inc(v_ones, 1)

            def rest(it, c):
                n = tile_no(it, c)
                pool.wait_ge(a_stats, n + 1)
                steps = [0]

                def link(ins):
                    steps[0] += 1
                    ins.then_inc(a_pool_step, 1)
                    pool.wait_ge(a_pool_step, n * 6 + steps[0])
                rstd_chain(pool, link, mv[:, TILES:TILES + 1, :], rs[:, TILES:TILES + 1, :]).then_inc(a_rstd, 1)

            def normalise(it, c):
                n = tile_no(it, c)
                pool.wait_ge(a_rec, n + 1)
                wait(pool, a_vl, n)
                pool.tensor_tensor(out=vals[:, :], in0=nd[:, 0, :], in1=nd[:, 1, :], op=ALU.mult).then_inc(a_vals, 1)

            def vals_lo(it, c):
                n = tile_no(it, c)
                pool.wait_ge(a_vh, n + 1)
                pool.tensor_tensor(out=vh[:, 1, :], in0=vals[:, :], in1=vh[:, 0, :].bitcast(f32), op=ALU.subtract)\
                    .then_inc(a_vl, 1)

            def xa_lo(it, c):
                n = tile_no(it, c)
                pool.wait_ge(a_xah, n + 1)
                pool.tensor_tensor(out=xa[:, 1, :], in0=xa_f[:, :], in1=xa[:, 0, :].bitcast(f32), op=ALU.subtract)\
                    .then_inc(a_xal, 1)

            def residual(it, c):
                n = tile_no(it, c)
                pool.wait_ge(a_oA, n + 1)
                xt = x_sb[:, ds(n, 1), :].rearrange("p a d -> p (a d)")
                pool.tensor_tensor(out=oA[:, :], in0=oA[:, :], in1=bo_sb[:, :], op=ALU.add).then_inc(a_ob, 1)
                pool.wait_ge(a_ob, n + 1)
                pool.tensor_tensor(out=xt, in0=xt, in1=oA[:, :], op=ALU.add).then_inc(a_x, 1)

            def turn(it, c):
                ok = lambda n: it is not None or 0 <= n < TILES
                if it is None and c == TILES:
                    rstd_pool(pool, st, 1, 0)
                if ok(c - 2):
                    normalise(it, c - 2)
                    vals_lo(it, c - 2)
                if ok(c + 4):
                    rest(it, c + 4)
                if ok(c - 2):
                    residual(it, c - 2)
                if ok(c + 4):
                    xa_lo(it, c + 4)
            for_turns(pool, turn)

        def scalar_program(act):
            act.wait_ge(small_loaded, 64)
            act.activation(w_qk[:, :, 0, :], w_small[:, 0:2 * D].rearrange("p (k d) -> p k d", k=2), ACT.Copy).then_inc(small_hi, 1)
            act.activation(w_o[:, 0:D], w_small[:, 2 * D:3 * D], ACT.Copy).then_inc(small_hi, 1)
            act.activation(w_r[:, 0:E], w_small[:, 4 * D:4 * D + E], ACT.Copy).then_inc(small_hi, 1)
            for f in range(2):
                if f == 0:
                    split_act(act, f, 0)
                split_act(act, f, 1)
                if f == 0:
                    for e in range(2):
                        high_part(act, e)
                route_act(act, f)
                if f == 0:
                    for e in range(2, E):
                        high_part(act, e)
                slots_act(act, f)
                if f == 0:
                    attention_act(act)

        def high_part(act, e):
            r = e % 4
            act.wait_ge(w_raw[r], e // 4 * 32 + 32)
            we = w_exp[:, e, :]
            act.activation(we[:, 0:2048].rearrange("p (k h f) -> p k h f", k=2, h=2)[:, :, 0, :],
                           stage[:, r, 0:1024].rearrange("p (k f) -> p k f", k=2), ACT.Copy)
            act.activation(we[:, 2048:3072].rearrange("p (c h d) -> p c h d", c=4, h=2)[:, :, 0, :],
                           stage[:, r, 1024:1536].rearrange("p (c d) -> p c d", c=4), ACT.Copy).then_inc(w_hi_done, 1)

        def split_act(act, f, batch):
            q = ffn[f]
            for i in range(*BATCHES[batch]):
                act.wait_ge(q.xT, i + 1)
                wait(act, q.logit, i - 1)
                act.activation(xr_h[i % 2], SB[i % 2][:, :], ACT.Copy).then_inc(q.xhi, 1)

        def route_act(act, f):
            q = ffn[f]
            act.wait_ge(q.logit, GROUPS)
            act.activation(lgB[:, :, :], logit_p[:, :, 1, :], ACT.Copy).then_inc(q.lgB, 1)
            act.wait_ge(q.gap, 1)
            act.activation(e2[:, :], e2[:, :], ACT.Exp).then_inc(q.exp2, 1)

        def slots_act(act, f):
            q = ffn[f]

            def turn(it, c):
                ok = lambda n: it is not None or 0 <= n < SLOTS
                j = slot_no(it, c)
                if ok(c + 1):
                    act.wait_ge(q.xgT, j + 2)
                    wait(act, q.up, j)
                    act.activation(xg_h[:, (c + 1) % 2, :], xg_p, ACT.Copy).then_inc(q.xgh, 1)
                if ok(c):
                    act.wait_ge(q.gate, j + 1)
                    wait(act, q.h, j - 1)
                    act.activation(s_act[:, c % 2, :], gate_p[c % 2], ACT.Silu).then_inc(q.silu, 1)
                if ok(c - 1):
                    act.wait_ge(q.hT, j)
                    wait(act, q.outp, j - 2)
                    act.activation(hT_h[:, (c - 1) % 2, :], hT_p[(c - 1) % 2], ACT.Copy).then_inc(q.hTh, 1)
                if ok(c - 2):
                    act.wait_ge(q.outp, j - 1)
                    wait(act, q.y, j - 2)
                    act.activation(yB[:, :], y_p[:, D:2 * D], ACT.Copy).then_inc(q.yB, 1)
            slot_turns(act, turn)

        def slot_turns(eng, turn):
            for c in range(-1, 4):
                turn(None, c)
            with eng.Fori(0, SLOTS // RING - 1) as it:
                for c in range(4, 4 + RING):
                    turn(it, c)
            for c in range(SLOTS - 4, SLOTS + 2):
                turn(None, c)

        def attention_act(act):
            def exps(it, c, k):
                n, cp, b = tile_no(it, c), k // NB, k % NB
                act.wait_ge(a_st, n * 8 + k + 1)
                wait(act, a_pv, n * 2 + cp - 1)
                act.activation(prob[:, cp, b, :, :].rearrange("p c s -> p (c s)"), ST[k % 2][:, :], ACT.Exp,
                               scale=HD ** -0.5).then_inc(a_exp, 1)

            def fill_kz(it, c, b):
                n, r = tile_no(it, c), c % 4
                act.wait_ge(a_stacked[r], quarter_no(it, c) * 16 + 16)
                wait(act, a_st, n * 8 + b - 3)
                rows = slice(32 * b, 32 * b + KROWS + 1)
                act.activation(kz[rows, b, :], k_st(r)[rows, :].bitcast(f32), ACT.Copy).then_inc(a_kz, 1)

            def negm(it, c):
                n = tile_no(it, c)
                act.wait_ge(a_mT, n + 1)
                wait(act, a_mhop, n * 16)
                act.activation(neg_m[:, :], MISC[0:NB * NC, 0:P], ACT.Copy, scale=-1.0).then_inc(a_negm, 1)

            def xa_evac(it, c):
                n = tile_no(it, c)
                act.wait_ge(a_xT, n + 1)
                wait(act, a_vp, n)
                act.activation(xa_f[:, :], MISC[:, 0:P], ACT.Copy)
                act.activation(xa[:, 0, :], MISC[:, 0:P], ACT.Copy).then_inc(a_xah, 1)

            def qk_evac(it, c):
                n = tile_no(it, c)
                act.wait_ge(a_qk, n + 1)
                wait(act, a_hop, n * 96)
                for k in range(2):
                    ins = act.activation(qk_hl[:, k, 0, :], MISC[:, P * (k + 1):P * (k + 2)], ACT.Identity,
                                         bias=bqk_sb[:, k:k + 1])
                ins.then_inc(a_qkh, 1)

            def o_evac(it, c):
                n = tile_no(it, c)
                act.wait_ge(a_pv, n * 2 + 2)
                wait(act, a_ohop, n * 16)
                act.activation(o_sb[:, :], PVB[:, :], ACT.Copy).then_inc(a_o, 1)

            def vals_hi(it, c):
                n = tile_no(it, c)
                act.wait_ge(a_vals, n + 1)
                wait(act, a_op, n)
                act.activation(vh[:, 0, :], vals[:, :], ACT.Copy).then_inc(a_vh, 1)

            def op_evac(it, c):
                n = tile_no(it, c)
                act.wait_ge(a_op, n + 1)
                wait(act, a_oA, n)
                act.activation(oB[:, :], PVB[:, P:2 * P], ACT.Copy).then_inc(a_oB, 1)

            def turn(it, c):
                ok = lambda n: it is not None or 0 <= n < TILES
                if it is None and c == TILES + 1:
                    split_act(act, 1, 0)
                for k in range(8):
                    if k == 1 and ok(c + 1):
                        negm(it, c + 1)
                    if k == 6 and ok(c + 4):
                        xa_evac(it, c + 4)
                    if k == 7 and ok(c + 4):
                        qk_evac(it, c + 4)
                    if ok(c):
                        exps(it, c, k)
                    if k < 2 and ok(c):
                        fill_kz(it, c, k + 2)
                    if 4 <= k < 6 and ok(c + 1):
                        fill_kz(it, c + 1, k - 4)
                    if k == 1 and ok(c - 2):
                        vals_hi(it, c - 2)
                    if k == 2 and ok(c - 1):
                        o_evac(it, c - 1)
                    if k == 3 and ok(c - 2):
                        op_evac(it, c - 2)
            for_turns(act, turn)

        def vector_program(dve):
            st = Steps(dve, dve_step)
            for f in range(2):
                if f == 0:
                    dve.wait_ge(x_loaded, 16)
                    for i in range(GROUPS):
                        stats_dve(dve, st, i).then_inc(ffn[0].stats, 1)
                    dve.wait_ge(const_ready, 1)
                    dve.wait_ge(small_hi, 3)
                    dve.tensor_tensor(w_qk[:, :, 1, :], w_small[:, 0:2 * D].rearrange("p (k d) -> p k d", k=2),
                                      w_qk[:, :, 0, :].bitcast(f32), ALU.subtract)
                    dve.tensor_tensor(w_o[:, D:2 * D], w_small[:, 2 * D:3 * D], w_o[:, 0:D].bitcast(f32), ALU.subtract)
                    dve.tensor_tensor(w_r[:, E:2 * E], w_small[:, 4 * D:4 * D + E], w_r[:, 0:E].bitcast(f32),
                                      ALU.subtract).then_inc(small_done, 1)
                    norm_dve(dve, 0, 0)
                else:
                    dve.wait_ge(a_x, TILES)
                    stats_dve(dve, st, GROUPS - 1).then_inc(ffn[1].stats, 1)
                norm_dve(dve, f, 1)
                route_dve(dve, st, f)
                slots_dve(dve, f)
                if f == 0:
                    attention_dve(dve, st)
            q = ffn[1]
            for n in range(TILES):
                for k in range(2):
                    combine(dve, 1, n, 2, n // 4, k)

        def combine(dve, f, n, turn_no, r, k):
            q = ffn[f]
            if k == 0:
                dve.wait_ge(q.gathered[r], turn_no * 16)
            else:
                dve.wait_ge(q.half, n + 1)
            xt = x_sb[:, ds(n, 1), :].rearrange("p a d -> p (a d)")
            w = wts[:, ds(n, 1), :].rearrange("p a k -> p (a k)")
            y = yg[:, r, k, :] if f == 0 else y_all[:, ds(n, 1), k, :].rearrange("p a d -> p (a d)")
            dve.scalar_tensor_tensor(out=xt, in0=y, scalar=w[:, k:k + 1], in1=xt, op0=ALU.mult, op1=ALU.add)\
                .then_inc(q.combined if k else q.half, 1)

        def stats_dve(dve, st, i):
            for k in range(4):
                ins = dve.bn_stats(st6[:, 4 * i + k, :], x_sb[:, 4 * i + k, :])
            st.link(ins)
            for k in range(4):
                ins = dve.bn_aggr(mv[:, 4 * i + k, :], st6[:, 4 * i + k, :])
            return ins

        def norm_dve(dve, f, batch):
            q = ffn[f]
            first, last = BATCHES[batch]
            dve.wait_ge(q.rstd, batch + 1)
            for i in range(first, last + 1):
                if i < last:
                    for k in range(4):
                        n = 4 * i + k
                        ins = dve.tensor_scalar(out=xn_all[:, n, 0:D], in0=x_sb[:, n, :], scalar1=mv[:, n, 0:1],
                                                scalar2=rs[:, n, 3:4], op0=ALU.subtract, op1=ALU.mult)
                    ins.then_inc(q.xn, 1)
                if i > first:
                    r = (i - 1) % 2
                    dve.wait_ge(q.xhi, i)
                    dve.tensor_tensor(xr_l[r], SB[r][:, :], xr_h[r].bitcast(f32), ALU.subtract).then_inc(q.xlo, 1)

        def route_dve(dve, st, f):
            q = ffn[f]
            link = st.link
            if f == 0:
                low_part(dve, 0).then_inc(w_lo_dve, 1)
            dve.wait_ge(q.lgB, 1)
            dve.tensor_tensor(lg[:, :, :], logit_p[:, :, 0, :], lgB[:, :, :], ALU.add).then_inc(q.lg, 1)
            dve.wait_ge(q.lg, 1)
            te = [P, TILES, E]
            wide = lambda a: a.unsqueeze(2).to_broadcast(te)
            rev_b = rev[:, :].unsqueeze(1).to_broadcast(te)

            def first_of_max(logits, m, one):
                link(dve.tensor_reduce(m[:, :], logits, X, ALU.max))
                link(dve.tensor_tensor(r1[:, :, :], logits, wide(m[:, :]), ALU.is_equal))
                link(dve.tensor_tensor(r1[:, :, :], r1[:, :, :], rev_b, ALU.mult))
                link(dve.tensor_reduce(kk[:, :], r1[:, :, :], X, ALU.max))
                link(dve.tensor_tensor(one[:, :, :], r1[:, :, :], wide(kk[:, :]), ALU.is_equal))

            first_of_max(lg[:, :, :], m1, one1)
            link(dve.scalar_tensor_tensor(out=r2[:, :, :], in0=one1[:, :, :], scalar=-3e38, in1=lg[:, :, :],
                                          op0=ALU.mult, op1=ALU.add))
            first_of_max(r2[:, :, :], m2, one2)
            dve.tensor_tensor(e2[:, :], m2[:, :], m1[:, :], ALU.subtract).then_inc(q.gap, 1)
            dve.tensor_tensor(sel[:, :, :], one1[:, :, :], one2[:, :, :], ALU.add).then_inc(q.sel, 1)
            if f == 0:
                low_part(dve, 1).then_inc(w_lo_dve, 1)
            dve.wait_ge(q.exp2, 1)
            link(dve.tensor_scalar(out=kk[:, :], in0=e2[:, :], scalar1=1.0, scalar2=2.0, op0=ALU.add, op1=ALU.mult))
            link(dve.reciprocal(wts[:, :, 0], kk[:, :]))
            link(dve.tensor_tensor(wts[:, :, 1], wts[:, :, 0], e2[:, :], ALU.mult))
            dve.wait_ge(q.rank, 1)
            link(dve.tensor_copy(n_e[:, :], MISC[:, 128:128 + E]))
            link(dve.tensor_tensor(cmp[:, :, :], thr[:, :].unsqueeze(1).to_broadcast([P, E, TILES]),
                                   n_e[:, :].unsqueeze(2).to_broadcast([P, E, TILES]), ALU.is_lt))
            link(dve.tensor_reduce(sl_e[:, :], cmp[:, :, :], X, ALU.add))
            link(dve.tensor_tensor(mm[:, :, :], before[:, :, :], sl_e[:, :].unsqueeze(1).to_broadcast([P, E, E]), ALU.mult))
            link(dve.tensor_reduce(off[:, :], mm[:, :, :], X, ALU.add))
            dve.tensor_tensor(incl[:, :], off[:, :], sl_e[:, :], ALU.add)
            link(dve.tensor_scalar(out=offs[:, :], in0=off[:, :], scalar1=float(P), scalar2=None, op0=ALU.mult))
            link(dve.tensor_tensor(r1[:, :, :], MISC[:, 0:P].rearrange("p (n e) -> p n e", e=E),
                                   offs[:, :].unsqueeze(1).to_broadcast(te), ALU.add))
            dve.tensor_tensor(r2[:, :, :], r1[:, :, :], one1[:, :, :], ALU.mult)
            link(dve.tensor_tensor(r1[:, :, :], r1[:, :, :], one2[:, :, :], ALU.mult))
            dve.tensor_reduce(posf[:, :, 0], r2[:, :, :], X, ALU.add)
            link(dve.tensor_reduce(posf[:, :, 1], r1[:, :, :], X, ALU.add))
            posm = posf[:, :, :].rearrange("p n k -> p (n k)")
            mj = [P, COPIES, SLOTS + 1]
            link(dve.tensor_tensor(ge, thr_j[:, :].unsqueeze(1).to_broadcast(mj), posm.unsqueeze(2).to_broadcast(mj),
                                   ALU.is_le))
            link(dve.tensor_reduce(slot_at[:, :], ge, X, ALU.add))
            link(dve.scalar_tensor_tensor(out=row_at[:, :], in0=slot_at[:, :], scalar=-float(P), in1=posm,
                                          op0=ALU.mult, op1=ALU.add))
            link(dve.tensor_tensor(hot_j[:, :, 1, :], ge[:, :, 0:SLOTS], ge[:, :, 1:SLOTS + 1], ALU.subtract))
            link(dve.tensor_tensor(hot_j[:, :, 0, :], hot_j[:, :, 1, :],
                                   no_a[:, :, :].rearrange("p n k -> p (n k)").unsqueeze(2).to_broadcast([P, COPIES, SLOTS]),
                                   ALU.mult))
            dve.tensor_scalar(out=hot_j[:, :, 1, :], in0=hot_j[:, :, 1, :], scalar1=no_p[:, 0:1], scalar2=None, op0=ALU.mult)
            dve.wait_ge(q.rows, 32)
            mr = [P, COPIES // 4, P]
            for part in range(0, COPIES, COPIES // 4):
                m = slice(part, part + COPIES // 4)
                dve.tensor_tensor(hot_r[:, m, :], row_at[:, m].unsqueeze(2).to_broadcast(mr),
                                  col[:, :].unsqueeze(1).to_broadcast(mr), ALU.is_equal).then_inc(q.hot, 1)
            if f == 0:
                low_part(dve, 7).then_inc(w_lo_dve, 1)
            link(dve.tensor_tensor(se[:, :, :], incl[0:1, :].unsqueeze(1).to_broadcast([1, SLOTS, E]),
                                   slot_j[:, :].unsqueeze(2).to_broadcast([1, SLOTS, E]), ALU.is_le))
            link(dve.tensor_reduce(sef[:, :], se[:, :, :], X, ALU.add))
            link(dve.tensor_scalar(out=sef[:, :], in0=sef[:, :], scalar1=float(E - 1), scalar2=float(WE),
                                   op0=ALU.min, op1=ALU.mult))
            dve.tensor_copy(slot_w[:, :], sef[:, :]).then_inc(q.slotw, 1)
            dve.wait_ge(q.inv, 1)
            link(dve.tensor_copy(idx_f[:, 1, :], MISC[:, SLOTS:2 * SLOTS]))
            dve.scalar_tensor_tensor(out=idx_f[:, 1, :], in0=MISC[:, 0:SLOTS], scalar=float(P), in1=idx_f[:, 1, :],
                                     op0=ALU.mult, op1=ALU.add)
            link(dve.scalar_tensor_tensor(out=idx_f[:, 0, :], in0=MISC[:, 0:SLOTS], scalar=0.0, in1=pad_no[:, :],
                                          op0=ALU.is_equal, op1=ALU.mult))
            link(dve.scalar_tensor_tensor(out=idx_f[:, 0, :], in0=idx_f[:, 1, :], scalar=float(PADS - P), in1=idx_f[:, 0, :],
                                          op0=ALU.add, op1=ALU.add))
            dve.tensor_copy(idx[:, SLOTS:SLOTS + 1], idx_f[:, 0, 0:1])
            dve.tensor_copy(idx[:, 0:SLOTS], idx_f[:, 0, :]).then_inc(q.idx, 1)

        def slots_dve(dve, f):
            q = ffn[f]

            def turn(it, c):
                ok = lambda n: it is not None or 0 <= n < SLOTS
                j = slot_no(it, c)
                if ok(c + 1):
                    dve.wait_ge(q.xgh, j + 2)
                    dve.tensor_tensor(xg_l[:, (c + 1) % 2, :], xg_p, xg_h[:, (c + 1) % 2, :].bitcast(f32),
                                      ALU.subtract).then_inc(q.xgl, 1)
                if ok(c):
                    dve.wait_ge(q.silu, j + 1)
                    dve.wait_ge(q.up, j + 1)
                    wait(dve, q.hT, j - 1)
                    dve.tensor_tensor(h_act[:, c % 2, :], up_p[c % 2], s_act[:, c % 2, :], ALU.mult).then_inc(q.h, 1)
                if ok(c - 1):
                    dve.wait_ge(q.hTh, j)
                    dve.tensor_tensor(hT_l[:, (c - 1) % 2, :], hT_p[(c - 1) % 2], hT_h[:, (c - 1) % 2, :].bitcast(f32),
                                      ALU.subtract).then_inc(q.hTl, 1)
                if ok(c - 2):
                    dve.wait_ge(q.yB, j - 1)
                    wait(dve, q.stored[c % 2], slot_half_no(it, c - 2) * 16)
                    dve.tensor_tensor(y_out[:, c % 2, :], y_p[:, 0:D], yB[:, :], ALU.add).then_inc(q.y, 1)
            slot_turns(dve, turn)

        def attention_dve(dve, st):
            def combined(it, c, k):
                combine(dve, 0, tile_no(it, c), half_no(it, c) + 1, c % 2, k)

            def stats(it, c):
                n = tile_no(it, c)
                wait_apart(dve, ffn[0].combined, n + 1, const_ready)
                dve.bn_stats(st6[:, TILES, :], x_sb[:, ds(n, 1), :].rearrange("p a d -> p (a d)")).then_inc(a_bn, 1)

            def moments(it, c):
                wait_apart(dve, a_bn, tile_no(it, c) + 1, const_ready)
                dve.bn_aggr(mv[:, TILES, :], st6[:, TILES, :]).then_inc(a_stats, 1)

            def xn(it, c):
                n = tile_no(it, c)
                dve.wait_ge(a_rstd, n + 1)
                dve.tensor_scalar(out=xn_t[:, c % 2, :], in0=x_sb[:, ds(n, 1), :].rearrange("p a d -> p (a d)"),
                                  scalar1=mv[:, TILES, 0:1], scalar2=rs[:, TILES, 3:4], op0=ALU.subtract, op1=ALU.mult)\
                    .then_inc(a_xn, 1)

            def qk_lo(it, c):
                n = tile_no(it, c)
                dve.wait_ge(a_qkh, n + 1)
                for k in range(2):
                    ins = dve.scalar_tensor_tensor(out=qk_hl[:, k, 1, :], in0=MISC[:, P * (k + 1):P * (k + 2)],
                                                   scalar=bqk_sb[:, k:k + 1], in1=qk_hl[:, k, 0, :].bitcast(f32),
                                                   op0=ALU.add, op1=ALU.subtract)
                ins.then_inc(a_qkl, 1)

            def v_add(it, c):
                n = tile_no(it, c)
                dve.wait_ge(a_vp, n + 1)
                if it is None and n == 0:
                    dve.wait_ge(v_ones, 1)
                wait(dve, a_pv, n * 2 - 6 if not isinstance(n, int) or n >= 4 else 0)
                dve.tensor_tensor(v_st[:, c % 4, :, :, 0:HD],
                                  MISC[:, 3 * P:4 * P].rearrange("p (b c d) -> p b c d", b=NB, c=NC),
                                  bv_sb[:, :].rearrange("p (c d) -> p c d", c=NC).unsqueeze(1).to_broadcast([P, NB, NC, HD]),
                                  ALU.add).then_inc(a_v, 1)

            def row_max(it, c, u):
                n = tile_no(it, c)
                dve.wait_ge(a_s, n * 16 + u + 1)
                dve.tensor_reduce(mx[:, c % 2, u:u + 1], SB[u % 2][:, :], X, ALU.max).then_inc(a_max, 1)

            def reciprocals(it, c):
                n = tile_no(it, c)
                dve.wait_ge(a_nd, n * 32 + 32)
                dve.reciprocal(nd[:, 1, :], nd[:, 1, :]).then_inc(a_rec, 1)

            def project(it, c):
                n = tile_no(it, c)
                dve.wait_ge(a_oB, n + 1)
                wait(dve, a_x, n)
                dve.tensor_tensor(oA[:, :], PVB[:, 0:P], oB[:, :], ALU.add).then_inc(a_oA, 1)

            def turn(it, c):
                ok = lambda n: it is not None or 0 <= n < TILES
                if it is None and 12 <= c < 15:
                    dve.wait_ge(a_x, 4 * (c - 11))
                    stats_dve(dve, st, c - 12).then_inc(ffn[1].stats, 1)
                if it is None and c == TILES + 1:
                    dve.wait_ge(a_pv, 2 * TILES)
                    norm_dve(dve, 1, 0)
                for u in range(16):
                    if ok(c + 2):
                        row_max(it, c + 2, u)
                    if u == 0 and ok(c - 2):
                        reciprocals(it, c - 2)
                    if ok(c + 4):
                        if u in (2, 3):
                            combined(it, c + 4, u - 2)
                        if u == 4:
                            stats(it, c + 4)
                        if u == 5:
                            moments(it, c + 4)
                    if u == 6 and ok(c + 3):
                        v_add(it, c + 3)
                    if u == 8 and ok(c - 2):
                        project(it, c - 2)
                    if ok(c + 4):
                        if u == 9:
                            xn(it, c + 4)
                        if u == 15:
                            qk_lo(it, c + 4)
            for_turns(dve, turn)

        def tensor_program(pe):
            pe.wait_ge(const_ready, 1)
            for f in range(2):
                route_pe(pe, f)
                slots_pe(pe, f)
                if f == 0:
                    attention_pe(pe)

        def logits_pe(pe, f, batch):
            q = ffn[f]
            first, last = BATCHES[batch]
            for i in range(first, last + 1):
                if i < last:
                    pe.wait_ge(q.xn, i + 1)
                    wait(pe, q.xlo, i - 1)
                    for k in range(4):
                        ins = pe.transpose(SB[i % 2][:, P * k:P * (k + 1)], xn_all[:, 4 * i + k, 0:D], ident[:, :])
                    ins.then_inc(q.xT, 1)
                if i > first:
                    pe.wait_ge(q.xlo, i)
                    if i == 1 and f == 0:
                        pe.wait_ge(small_done, 1)
                    for k in range(4):
                        n = 4 * (i - 1) + k
                        for part, src in enumerate((xr_h, xr_l)):
                            ins = pe.matmul(MISC[:, 256 + 16 * n:256 + 16 * n + 16], src[(i - 1) % 2][:, P * k:P * (k + 1)],
                                            w_r[:, :], start=(part == 0), stop=(part == 1))
                    ins.then_inc(q.logit, 1)

        def route_pe(pe, f):
            q = ffn[f]
            if f == 0:
                logits_pe(pe, f, 0)
            logits_pe(pe, f, 1)
            pe.wait_ge(q.sel, 1)
            flat = sel[:, :, :].rearrange("p n e -> p (n e)")
            pe.matmul(MISC[:, 0:P], upper[:, :], flat, start=True, stop=False)
            for s in range(1, TILES):
                pe.matmul(MISC[:, E * s:P], ones_b[:, :], flat[:, 0:P - E * s], start=False, stop=(s == TILES - 1))
            for n in range(TILES):
                ins = pe.matmul(MISC[:, P:P + E], ones_b[:, :], flat[:, E * n:E * n + E], start=(n == 0), stop=(n == TILES - 1))
            ins.then_inc(q.rank, 1)
            for m in range(COPIES):
                if m % (COPIES // 4) == 0:
                    pe.wait_ge(q.hot, m // (COPIES // 4) + 1)
                ins = pe.matmul(MISC[:, 0:2 * SLOTS], hot_r[:, m, :], hot_j[:, m, :, :].rearrange("p h j -> p (h j)"),
                                start=(m == 0), stop=(m == COPIES - 1))
            ins.then_inc(q.inv, 1)

        def slots_pe(pe, f):
            q = ffn[f]
            pe.wait_ge(q.slotw, 1)
            pe.wait_ge(w_lo_dve, len(LO_DVE))
            pe.wait_ge(w_lo_pool, len(LO_POOL))
            flat = w_exp[:, :, :].rearrange("p e c -> p (e c)")
            w_col = {}

            def turn(it, c):
                ok = lambda n: it is not None or 0 <= n < SLOTS
                j = slot_no(it, c)
                if c % 4 == 0:
                    lo, hi = (c - 4, c + 4) if it is not None else (max(c - 4, 0), min(c + 4, SLOTS))
                    _, vals_ = nc.values_load_multi_w_load_instructions(
                        slot_w[0:1, ds(slot_no(it, lo), hi - lo)], engines=[mybir.EngineType.PE], min_val=0, max_val=WE * (E - 1),
                        skip_runtime_bounds_check_because="slot_w is min(., E - 1) * WE")
                    w_col.update(zip(range(lo, hi), vals_))
                w_up, w_down = w_col.get(c), w_col.get(c - 2)
                if ok(c):
                    wait(pe, q.xgl, j + 1)
                if ok(c + 1):
                    pe.wait_ge(q.xg[(c + 1) % RING], slot_ring_no(it, c + 1) * 16 + 16 + q.xg_base)
                    pe.transpose(xg_p, xg[:, (c + 1) % RING, :], ident[:, :]).then_inc(q.xgT, 1)
                if ok(c):
                    xh, xl = xg_h[:, c % 2, :], xg_l[:, c % 2, :]
                    for dst, free, done, base in ((gate_p[c % 2], q.silu, q.gate, 0), (up_p[c % 2], q.h, q.up, 1024)):
                        wait(pe, free, j - 1)
                        pe.matmul(dst, xh, flat[:, ds(w_up + base, F)], start=True, stop=False)
                        pe.matmul(dst, xh, flat[:, ds(w_up + (base + F), F)], start=False, stop=False)
                        pe.matmul(dst, xl, flat[:, ds(w_up + base, F)], start=False, stop=True).then_inc(done, 1)
                if ok(c - 1):
                    pe.wait_ge(q.h, j)
                    wait(pe, q.hTl, j - 2)
                    r = (c - 1) % 2
                    for k in range(4):
                        ins = pe.transpose(hT_p[r][:, P * k:P * (k + 1)], h_act[:, r, P * k:P * (k + 1)], ident[:, :])
                    ins.then_inc(q.hT, 1)
                if ok(c - 2):
                    pe.wait_ge(q.hTl, j - 1)
                    wait(pe, q.y, j - 2)
                    r = c % 2
                    for k in range(4):
                        for part, src in enumerate((hT_h, hT_l)):
                            ins = pe.matmul(y_p, src[:, r, P * k:P * (k + 1)], flat[:, ds(w_down + (2048 + 256 * k), 2 * D)],
                                            start=(k == 0 and part == 0), stop=(k == 3 and part == 1))
                    ins.then_inc(q.outp, 1)
            slot_turns(pe, turn)

        def attention_pe(pe):
            def cols(t, b, c=None):
                t = t[:, b, :]
                return t if c is None else t[:, P * c:P * (c + 1)]

            def scores_for_max(it, c, u):
                n, r = tile_no(it, c), c % 4
                b, ch = u // NC, u % NC
                if ch == 0:
                    if b == 0:
                        pe.wait_ge(a_stacked[r], quarter_no(it, c) * 16 + 16)
                    pe.wait_ge(a_qz[b], n * 16 + 16)
                wait(pe, a_max, n * 16 + u - 1)
                pe.matmul(SB[u % 2][:, :], qz[:, b, P * ch:P * (ch + 1)], k_st(r), start=True, stop=True).then_inc(a_s, 1)

            def scores(it, c, k):
                n, r = tile_no(it, c), c % 4
                cp, b = k // NB, k % NB
                if k == 0:
                    pe.wait_ge(a_mrow[r], quarter_no(it, c) * 64 + 64)
                if cp == 0:
                    pe.wait_ge(a_kz, n * NB + b + 1)
                wait(pe, a_exp, n * 8 + k - 1)
                for cc in range(2):
                    ch = 2 * cp + cc
                    ins = pe.matmul(ST[k % 2][:, 512 * cc:512 * (cc + 1)], kz[:, b, P * ch:P * (ch + 1)], q_st(r),
                                    start=True, stop=True)
                ins.then_inc(a_st, 1)

            def values(it, c, cp, cc):
                n = tile_no(it, c)
                if cc == 0:
                    pe.wait_ge(a_exp, n * 8 + 4 * cp + 4)
                if cp == 0 and cc == 0:
                    pe.wait_ge(a_v, n + 1)
                    wait(pe, a_o, n)
                    wait(pe, a_oA, n - 1)
                for b in range(NB):
                    ins = pe.matmul(PVB[32 * b:32 * b + 32, :], v_st[:, c % 4, b, 2 * cp + cc, :], prob[:, cp, b, cc, :],
                                    start=(cp == 0 and cc == 0), stop=(cp == 1 and cc == 1))
                if cc == 1:
                    ins.then_inc(a_pv, 1)

            def max_t(it, c):
                n = tile_no(it, c)
                pe.wait_ge(a_max, n * 16 + 16)
                if it is not None or n + 2 < TILES:
                    pe.wait_ge(a_qkl, n + 3)
                else:
                    pe.wait_ge(a_negm, n)
                pe.transpose(MISC[0:NB * NC, 0:P], mx[:, c % 2, :], ident[:, :]).then_inc(a_mT, 1)

            def x_t(it, c):
                n = tile_no(it, c)
                pe.wait_ge(a_xn, n + 1)
                wait(pe, a_v, n)
                pe.transpose(MISC[:, 0:P], xn_t[:, c % 2, :], ident[:, :]).then_inc(a_xT, 1)

            def qk(it, c):
                n = tile_no(it, c)
                pe.wait_ge(a_xal, n + 1)
                for k in range(2):
                    o = MISC[:, P * (k + 1):P * (k + 2)]
                    pe.matmul(o, w_qk[:, k, 0, :], xa[:, 0, :], start=True, stop=False)
                    pe.matmul(o, w_qk[:, k, 0, :], xa[:, 1, :], start=False, stop=False)
                    ins = pe.matmul(o, w_qk[:, k, 1, :], xa[:, 0, :], start=False, stop=True)
                ins.then_inc(a_qk, 1)

            def v(it, c):
                n = tile_no(it, c)
                if it is not None or n >= 2:
                    pe.wait_ge(a_negm, n - 1)
                else:
                    pe.wait_ge(a_qkl, n + 1)
                wv = w_small[:, 3 * D:4 * D].rearrange("p (i c) -> p i c", i=GC)
                for b in range(NB):
                    for g in range(GC):
                        ins = pe.matmul(MISC[32 * g:32 * g + 32, 3 * P + 32 * b:3 * P + 32 * b + 32],
                                        xa_f[:, BLK * b:BLK * (b + 1)], wv[:, g, :], start=True, stop=True)
                ins.then_inc(a_vp, 1)

            def project(it, c):
                n = tile_no(it, c)
                pe.wait_ge(a_vl, n + 1)
                pe.wait_ge(a_o, n + 2 if it is not None or n + 1 < TILES else TILES)
                pe.matmul(PVB[:, 0:2 * P], vh[:, 0, :], w_o[:, :], start=True, stop=False)
                pe.matmul(PVB[:, 0:2 * P], vh[:, 1, :], w_o[:, :], start=False, stop=True).then_inc(a_op, 1)

            def turn(it, c):
                ok = lambda n: it is not None or 0 <= n < TILES
                if it is None and c == TILES + 1:
                    logits_pe(pe, 1, 0)
                for k in range(8):
                    if ok(c + 2):
                        scores_for_max(it, c + 2, 2 * k)
                    if k == 7 and ok(c + 4):
                        qk(it, c + 4)
                    if ok(c):
                        scores(it, c, k)
                    if ok(c + 2):
                        scores_for_max(it, c + 2, 2 * k + 1)
                    if k == 0 and ok(c + 1):
                        max_t(it, c + 1)
                    if k < 2 and ok(c - 1):
                        values(it, c - 1, 1, k)
                    if k == 2 and ok(c + 3):
                        v(it, c + 3)
                    if k == 3 and ok(c - 2):
                        project(it, c - 2)
                    if k in (5, 7) and ok(c):
                        values(it, c, 0, (5, 7).index(k))
                    if k == 5 and ok(c + 4):
                        x_t(it, c + 4)
            for_turns(pe, turn)

        block = ctx.enter_context(nc.Block())
        block.sync(sync_program)
        block.gpsimd(gpsimd_program)
        block.scalar(scalar_program)
        block.vector(vector_program)
        block.tensor(tensor_program)


_OUT_SHAPE = (B, S, D)


def kernel(**inputs):
    import numpy as np
    import concourse.bacc as bacc
    from concourse.bass_utils import run_bass_kernel_spmd as run

    nc = bacc.Bacc("TRN2", target_bir_lowering=False, num_devices=1)
    i = {k.replace("L0_", ""): np.asarray(v) for k, v in inputs.items()}
    w = i["attn_Wqkv"].reshape(G, 3, HD, D)
    b = i["attn_bqkv"].reshape(G, 3, HD)
    wq, wk = (w[:, k].transpose(2, 1, 0).reshape(D, D) for k in (0, 1))
    wo = i["attn_Wo"].reshape(D, G, HD).transpose(2, 1, 0).reshape(D, D)
    wv = w[:, 2].reshape(NC, GC, HD, D).transpose(3, 1, 0, 2).reshape(D, D)
    bv = b[:, 2].reshape(NC, GC, HD).transpose(1, 0, 2).reshape(GC, 1, NC * HD)
    arrays = {
        "x": i["attn_x"].reshape(B * S, D),
        "w_gate_up": np.stack([i["ffn_We_gate"], i["ffn_We_in"]], axis=1),
        "w_down": i["ffn_We_out"],
        "w_att": np.concatenate([wq, wk, wo, wv, i["ffn_W_gate"]], axis=1),
        "b_qk": b[:, 0:2].transpose(2, 0, 1).reshape(D, 2),
        "b_v": np.broadcast_to(bv, (GC, BLK, NC * HD)).reshape(P, NC * HD),
        "b_o": np.broadcast_to(i["attn_bo"][None, :], (P, D)),
    }
    arrays = {f"in_{k}": np.ascontiguousarray(v) for k, v in arrays.items()}
    f32 = mybir.dt.float32
    aps = {k: nc.dram_tensor(k, v.shape, f32, kind="ExternalInput").ap() for k, v in arrays.items()}
    out = nc.dram_tensor("out", (B * S, D), f32, kind="ExternalOutput").ap()
    scratch = [nc.dram_tensor(n, s, f32, kind="Internal").ap() for n, s in (
        ("x_tok", (PADS + 2 * B * S, D)), ("y_tok", (PADS + 2 * B * S, D)), ("qk_hop", (2, 2, P, S)),
        ("max_hop", (NB * NC, P)), ("att_hop", (P, S)))]
    macaron_kernel(nc, aps["in_x"], aps["in_w_gate_up"], aps["in_w_down"], aps["in_w_att"],
                   aps["in_b_qk"], aps["in_b_v"], aps["in_b_o"], out, *scratch)
    r = run(nc, [arrays], core_ids=[0])
    return r.results[0]["out"].reshape(_OUT_SHAPE)
```
